# Optimizing a Trainium2 kernel written in Bass

```python
import numpy as np
import jax
import jax.numpy as jnp

def _softmax(x, axis=-1):
    return jax.nn.softmax(x, axis=axis)

def _gelu(x):
    return jax.nn.gelu(x, approximate=True)

def _silu(x):
    return jax.nn.silu(x)

def _sigmoid(x):
    return jax.nn.sigmoid(x)

def _layernorm(x, axis=-1, eps=1e-05):
    m = jnp.mean(x, axis=axis, keepdims=True)
    v = jnp.var(x, axis=axis, keepdims=True)
    return (x - m) / jnp.sqrt(v + eps)

def _scatter_add(tgt, idx, src, axis=0):
    return tgt.at[idx].add(src)

def _segment_sum(src, seg, n):
    return jax.ops.segment_sum(src, seg, n)
kernel_name = 'mk_macaron_d1_jaxref_r8_ae141d'

def setup_inputs(seed: int=0):
    np.random.seed(seed)
    _w = jnp.asarray

    def _L0_attn_setup():
        import jax, jax.numpy as jnp
        import numpy as np
        B, T, D, H, R = (4, 512, 128, 16, 32)
        DH = D // H
        key = jax.random.key(seed)
        ks = jax.random.split(key, 5)
        s = 0.02
        return {'x': jax.random.normal(ks[0], (B, T, D), dtype=jnp.float32), 'Wq': jax.random.normal(ks[1], (D, D), dtype=jnp.float32) * s, 'bq': jnp.zeros((D,), dtype=jnp.float32), 'Wd': jax.random.normal(ks[2], (D, R), dtype=jnp.float32) * s, 'bd': jnp.zeros((R,), dtype=jnp.float32), 'Wu': jax.random.normal(ks[3], (R, 2 * D), dtype=jnp.float32) * s, 'bu': jnp.zeros((2 * D,), dtype=jnp.float32), 'Wo': jax.random.normal(ks[4], (D, D), dtype=jnp.float32) * s, 'bo': jnp.zeros((D,), dtype=jnp.float32)}
    _L0_attn_in = _L0_attn_setup()

    def _L0_ffn_setup():
        import jax, jax.numpy as jnp
        import numpy as np
        D_MODEL = 128
        D_FF = 512
        NUM_EXPERTS = 8
        TOP_K = 2
        BATCH = 4
        SEQ = 256
        key = jax.random.key(seed)
        ks = jax.random.split(key, 8)
        s = 0.02
        x = jax.random.normal(ks[0], (BATCH, SEQ, D_MODEL), dtype=jnp.float32)
        router_w = jax.random.normal(ks[1], (D_MODEL, NUM_EXPERTS), dtype=jnp.float32) * s
        router_b = jnp.zeros((NUM_EXPERTS,), dtype=jnp.float32)
        W1 = jax.random.normal(ks[2], (NUM_EXPERTS, D_MODEL, D_FF), dtype=jnp.float32) * s
        b1 = jnp.zeros((NUM_EXPERTS, D_FF), dtype=jnp.float32)
        W2 = jax.random.normal(ks[3], (NUM_EXPERTS, D_FF, D_MODEL), dtype=jnp.float32) * s
        b2 = jnp.zeros((NUM_EXPERTS, D_MODEL), dtype=jnp.float32)
        return {'x': x, 'router_w': router_w, 'router_b': router_b, 'W1': W1, 'b1': b1, 'W2': W2, 'b2': b2}
    _L0_ffn_in = _L0_ffn_setup()
    _d = {'L0_attn_x': _L0_attn_in['x'], 'L0_attn_Wq': _L0_attn_in['Wq'], 'L0_attn_bq': _L0_attn_in['bq'], 'L0_attn_Wd': _L0_attn_in['Wd'], 'L0_attn_bd': _L0_attn_in['bd'], 'L0_attn_Wu': _L0_attn_in['Wu'], 'L0_attn_bu': _L0_attn_in['bu'], 'L0_attn_Wo': _L0_attn_in['Wo'], 'L0_attn_bo': _L0_attn_in['bo'], 'L0_ffn_router_w': _L0_ffn_in['router_w'], 'L0_ffn_router_b': _L0_ffn_in['router_b'], 'L0_ffn_W1': _L0_ffn_in['W1'], 'L0_ffn_b1': _L0_ffn_in['b1'], 'L0_ffn_W2': _L0_ffn_in['W2'], 'L0_ffn_b2': _L0_ffn_in['b2']}
    _x0 = _d['L0_attn_x']
    _d['L0_attn_x'] = jax.random.normal(jax.random.fold_in(jax.random.key(seed), 1), (16, 256, 128), dtype=_x0.dtype)
    del _x0
    return _d

def reference(L0_attn_x, L0_attn_Wq, L0_attn_bq, L0_attn_Wd, L0_attn_bd, L0_attn_Wu, L0_attn_bu, L0_attn_Wo, L0_attn_bo, L0_ffn_router_w, L0_ffn_router_b, L0_ffn_W1, L0_ffn_b1, L0_ffn_W2, L0_ffn_b2):

    def _L0_attn_ref(x, Wq, bq, Wd, bd, Wu, bu, Wo, bo):
        import jax, jax.numpy as jnp
        import numpy as np
        B, T, D, H, R = (4, 512, 128, 16, 32)
        DH = D // H
        b, t = (x.shape[0], x.shape[1])
        q = (x @ Wq + bq).reshape(b, t, H, DH)
        kv = ((x @ Wd + bd) @ Wu + bu).reshape(b, t, H, 2 * DH)
        k, v = (kv[..., :DH], kv[..., DH:])
        q = jax.nn.elu(q) + 1.0
        k = jax.nn.elu(k) + 1.0
        context = jnp.einsum('bthd,bthe->bhde', k, v)
        out = jnp.einsum('bthd,bhde->bthe', q, context)
        k_sum = k.sum(axis=1)
        z = 1.0 / (jnp.einsum('bthd,bhd->bth', q, k_sum) + 1e-06)
        out = out * z[..., None]
        return out.reshape(b, t, D) @ Wo + bo

    def _L0_ffn_ref(x, router_w, router_b, W1, b1, W2, b2):
        import jax, jax.numpy as jnp
        import numpy as np
        D_MODEL = 128
        D_FF = 512
        NUM_EXPERTS = 8
        TOP_K = 2
        BATCH = 4
        SEQ = 256
        logits = jnp.einsum('bsd,de->bse', x, router_w) + router_b
        topk_scores, topk_idx = jax.lax.top_k(logits, TOP_K)
        topk_gates = jax.nn.softmax(topk_scores, axis=-1)
        onehot = jax.nn.one_hot(topk_idx, NUM_EXPERTS, dtype=x.dtype)
        combine = jnp.einsum('bsk,bske->bse', topk_gates, onehot)
        combine_e = jnp.moveaxis(combine, -1, 0)

        def expert_step(acc, params):
            w1, bb1, w2, bb2, c = params
            h = jax.nn.relu(jnp.einsum('bsd,df->bsf', x, w1) + bb1)
            y = jnp.einsum('bsf,fd->bsd', h, w2) + bb2
            return (acc + y * c[..., None], None)
        out, _ = jax.lax.scan(expert_step, jnp.zeros_like(x), (W1, b1, W2, b2, combine_e))
        return out
    x = L0_attn_x
    x = x + 0.5 * _L0_ffn_ref(_layernorm(x, axis=-1), L0_ffn_router_w, L0_ffn_router_b, L0_ffn_W1, L0_ffn_b1, L0_ffn_W2, L0_ffn_b2)
    x = x + _L0_attn_ref(_layernorm(x, axis=-1), L0_attn_Wq, L0_attn_bq, L0_attn_Wd, L0_attn_bd, L0_attn_Wu, L0_attn_bu, L0_attn_Wo, L0_attn_bo)
    x = x + 0.5 * _L0_ffn_ref(_layernorm(x, axis=-1), L0_ffn_router_w, L0_ffn_router_b, L0_ffn_W1, L0_ffn_b1, L0_ffn_W2, L0_ffn_b2)
    return x

_drawn_inputs = setup_inputs


def setup_inputs(seed=0):
    import zlib

    import numpy as np

    out = dict(_drawn_inputs(seed))
    spreads = {'L0_attn_bq': (0.0, 2.0),
     'L0_attn_bd': (0.0, 0.8),
     'L0_attn_bu': (0.0, 0.314),
     'L0_attn_bo': (0.0, 0.1),
     'L0_ffn_router_b': (0.0, 0.1),
     'L0_ffn_b1': (0.0, 0.372),
     'L0_ffn_b2': (0.0, 0.1)}
    factors = {'L0_attn_Wq': 22.752, 'L0_attn_Wd': 8.0, 'L0_attn_Wu': 8.0}
    for name, (base, spread) in spreads.items():
        noise = np.random.default_rng([zlib.crc32(name.encode()), seed]).standard_normal(out[name].shape)
        drawn = base * np.exp(spread * noise) if base else spread * noise
        out[name] = jnp.asarray(drawn.astype(out[name].dtype))
    for name, factor in factors.items():
        out[name] = (out[name] * factor).astype(out[name].dtype)
    return out
```

```python
import concourse.bass as bass
from concourse import mybir
from contextlib import ExitStack


def build_macaron_block(nc, x, Wq, bq, Wd, bd, Wu, bu, Wo, bo, router_w, router_b, W1, b1, W2, b2, out):
    fp32, f32r, bf16, i32 = mybir.dt.float32, mybir.dt.float32r, mybir.dt.bfloat16, mybir.dt.int32
    ALU, ACT, AX = mybir.AluOpType, mybir.ActivationFunctionType, mybir.AxisListType

    P = 128
    B, TB, D = x.shape
    NTOK = B * TB
    T = NTOK // P
    PT = TB // P
    UNITS = B
    E, F = b1.shape
    K = 2
    FC = F // P
    R = Wd.shape[1]
    HD = 8
    H = D // HD
    UNROLL = 4
    TILES_MOST = (NTOK * K + E * (P - 1)) // P
    S = -(-TILES_MOST // UNROLL) * UNROLL
    THR = NTOK // P
    LAG = 6
    GB = YB = 4
    BIG = 3.0e38

    x_rows = x.rearrange("b t d -> (b t) d")
    out_rows = out.rearrange("b t d -> (b t) d")
    xn_dram = nc.dram_tensor("normed_rows", (NTOK, D), fp32, kind="Internal").ap()
    y_dram = nc.dram_tensor("expert_rows", (K * NTOK, D), fp32, kind="Internal").ap()

    ctx = ExitStack()
    with ctx:
        def sb(name, shape, dt=fp32):
            return ctx.enter_context(nc.sbuf_tensor(name, shape, dt))

        def sem(name):
            return ctx.enter_context(nc.semaphore(name))

        X = sb("X", [P, T, D])
        Wraw = sb("Wraw", [P, 2, E * F // 2])
        W1h, W1l = sb("W1h", [P, E * F], f32r), sb("W1l", [P, E * F], f32r)
        W2h, W2l = sb("W2h", [P, E * F], f32r), sb("W2l", [P, E * F], f32r)
        b1_all = sb("b1_all", [P, E * F])
        b2_all = sb("b2_all", [P, E * D])
        rw = sb("rw", [P, E])
        rb = sb("rb", [P, E])
        wq = sb("wq", [P, D])
        wd = sb("wd", [P, R])
        wu_raw = sb("wu_raw", [R + 1, 2 * D])
        wu = sb("wu", [R + 1, 2, D])
        wo = sb("wo", [P, D])
        bo_row = sb("bo_row", [1, D])
        bq_col = sb("bq_col", [P, 1])
        bd_col = sb("bd_col", [R, 1])
        ident = sb("ident", [P, P])
        ones_bf = sb("ones_bf", [P, P], bf16)
        below = sb("below", [P, P], bf16)
        iota_lo = sb("iota_lo", [P, P], bf16)
        iota_hi = sb("iota_hi", [P, S], bf16)
        iota_s = sb("iota_s", [P, S])
        order = sb("order", [P, E])
        steps = sb("steps", [P, THR])
        part = sb("part", [P, 1])
        dest = sb("dest", [P, T, K])
        carry = sb("carry", [P, E, T])
        quarter = sb("quarter", [P, PT])
        minus_half = sb("minus_half", [P, PT])
        ones_e = sb("ones_e", [P, E])
        head_mask = sb("head_mask", [P, H, HD])
        ones_row = sb("ones_row", [1, P])
        norm = {}
        for n in "ra":
            norm[n] = dict(
                st=sb(f"st_{n}", [P, 2, PT, 6]), parts=sb(f"parts_{n}", [P, 2, 3, PT]),
                mean=sb(f"mean_{n}", [P, 2, PT]), dd=sb(f"dd_{n}", [P, 2, PT]), sq=sb(f"sq_{n}", [P, 2, PT]), vh=sb(f"vh_{n}", [P, 2, PT]),
                ve=sb(f"ve_{n}", [P, 2, PT]), rs=sb(f"rs_{n}", [P, 2, PT]),
                xn=sb(f"xn_{n}", [P, 2, PT, D]), xT=sb(f"xT_{n}", [P, 2, PT * P]),
                s_st=sem(f"stats_{n}"), s_parts=sem(f"stat_parts_{n}"), s_terms=sem(f"stat_terms_{n}"), s_sq=sem(f"stat_square_{n}"), s_ve=sem(f"var_eps_{n}"), s_rs=sem(f"rstd_{n}"), s_xn=sem(f"normed_{n}"),
                s_tp=sem(f"transposed_{n}"), s_xT=sem(f"xT_ready_{n}"))
        LG = sb("LG", [P, T, E])
        m1, m2 = sb("m1", [P, T]), sb("m2", [P, T])
        wa, wb, wc = sb("wa", [P, T, E]), sb("wb", [P, T, E]), sb("wc", [P, T, E])
        r12 = sb("r12", [P, 2, T])
        oh1, oh2 = sb("oh1", [P, T, E]), sb("oh2", [P, T, E])
        mask = sb("mask", [P, T, E], bf16)
        dm, ex, den, rden = sb("dm", [P, T]), sb("ex", [P, T]), sb("den", [P, T]), sb("rden", [P, T])
        gate = sb("gate", [P, K, T])
        cnt, cum = sb("cnt", [P, E * T]), sb("cum", [P, E * T])
        cmp_te = sb("cmp_te", [P, E, THR])
        tiles_e, tend, tstart = sb("tiles_e", [P, E]), sb("tend", [P, E]), sb("tstart", [P, E])
        off = sb("off", [P, E, T])
        pos = sb("pos", [P, T, E])
        slot_f = sb("slot_f", [P, T, K])
        slot_i, hi_i, lo_i = sb("slot_i", [P, T * K], i32), sb("hi_i", [P, T * K], i32), sb("lo_i", [P, T * K], i32)
        hi_f, lo_f = sb("hi_f", [P, T * K]), sb("lo_f", [P, T * K])
        cmp_s = sb("cmp_s", [P, S, E])
        eid_f = sb("eid_f", [P, S])
        eid = sb("eid", [P, S], i32)
        A = sb("A", [P, 4, P], bf16)
        Hh = sb("Hh", [P, 4, 2, S], bf16)
        tok_f = sb("tok_f", [P, S])
        idx_out, idx_in = sb("idx_out", [P, S], i32), sb("idx_in", [P, S], i32)
        xg = sb("xg", [P, GB, D])
        xh, xl = sb("xh", [P, 2, P], f32r), sb("xl", [P, 2, P], f32r)
        hb = sb("hb", [P, 2, F])
        hh, hl = sb("hh", [P, 2, F], f32r), sb("hl", [P, 2, F], f32r)
        yt = sb("yt", [P, YB, D])
        yb = sb("yb", [P, 2, K, PT, D])
        qe, qr, qT = sb("qe", [P, 2, PT * P]), sb("qr", [P, 2, PT * P]), sb("qT", [P, 2, PT * P])
        cT = sb("cT", [R + 1, 2, PT * P])
        ke, kr, kk = sb("ke", [P, 2, PT, D]), sb("kr", [P, 2, PT, D]), sb("kk", [P, 2, PT, D])
        v1 = sb("v1", [P, 2, PT, D + 1])
        cx = sb("cx", [P, 2, D])
        ks = sb("ks", [P, 2, D])
        zz, rz, oT = sb("zz", [P, 2, PT * P]), sb("rz", [P, 2, PT * P]), sb("oT", [P, 2, PT * P])

        bank = [ctx.enter_context(nc.psum_tensor(f"bank{i}", [P, 512], fp32)) for i in range(8)]

        s_x, s_w, s_wraw, s_bias = sem("x_loaded"), sem("small_weights"), [sem(f"W_part_loaded{c}") for c in range(4)], sem("biases")
        s_const = sem("constants")
        s_cz = sem("constants_cleared")
        s_wh, s_split = sem("W_high_parts"), sem("W_split")
        s_wu, s_fix = sem("wu_ready"), sem("fixed_ones")
        s_qc = sem("q_c_in_psum")
        s_pl, s_lg = sem("logits_in_psum"), sem("logits")
        norm["r"]["s_use"], norm["a"]["s_use"] = s_pl, s_qc
        s_xs = [sem(f"normed_stored{i}") for i in range(2)]
        s_rt = sem("routing_step")
        s_dm, s_ex = sem("gate_difference"), sem("gate_exp")
        s_mask, s_rank = sem("mask"), sem("ranks")
        s_oh, s_inv = sem("slot_onehots"), sem("slot_tokens")
        s_acc = sem("onehots_used")
        s_eid, s_idx = sem("expert_ids"), sem("indices")
        s_g = [sem(f"gathered{i}") for i in range(GB)]
        s_s = [sem(f"scattered{i}") for i in range(YB)]
        s_gT, s_xh, s_xl, s_up = sem("gathered_transposed"), sem("x_high"), sem("x_low"), sem("up_done")
        s_hb, s_hT, s_hh, s_hl = sem("hidden_biased"), sem("hidden_transposed"), sem("h_high"), sem("h_low")
        s_dn, s_y = sem("down_done"), sem("y_ready")
        s_yl = [sem(f"y_loaded{i}") for i in range(2)]
        s_c0, s_c1 = sem("first_choice_added"), sem("second_choice_added")
        s_qe, s_q, s_cT = sem("q_exp_relu"), sem("q"), sem("c")
        s_kv, s_ke, s_k = sem("k_v_in_psum"), sem("k_exp_relu_v"), sem("k")
        s_cp, s_cx = sem("context_in_psum"), sem("context")
        s_oz, s_zz, s_rz, s_oT = sem("out_z_in_psum"), sem("z_plus_eps"), sem("z_reciprocal"), sem("attn_out")
        s_pr, s_x2 = sem("projected"), sem("attn_added")
        s_out = sem("stored")

        def wait(eng, s, value):
            if not (isinstance(value, int) and value <= 0):
                eng.wait_ge(s, value)

        def w_part(of_W1, of_W2, c):
            return (of_W1 if c < 2 else of_W2)[:, (c % 2) * (E * F // 2):(c % 2 + 1) * (E * F // 2)]

        def pipeline(eng, count, unroll, stages):
            deepest = max(lag for lag, _ in stages)
            first = -(-(deepest + 1) // unroll) * unroll
            rounds = (count - first) // unroll

            def peeled(s):
                for lag, body in stages:
                    if 0 <= s - lag < count:
                        body(s - lag, (s - lag) % unroll, (s - lag) // unroll)

            for s in range(first):
                peeled(s)
            with eng.Fori(0, rounds) as i:
                for j in range(unroll):
                    for lag, body in stages:
                        n = first + j - lag
                        body(i * unroll + n, n % unroll, i + n // unroll)
            for s in range(first + rounds * unroll, count + deepest):
                peeled(s)

        block = ctx.enter_context(nc.Block())

        @block.sync
        def _(sp):
            for c in range(4):
                t0 = c * T // 4
                sp.dma_start(X[:, t0:t0 + T // 4, :], x_rows[t0 * P:(t0 + T // 4) * P, :].rearrange("(t p) d -> p t d", p=P)).then_inc(s_x, 16)
                if c == 0:
                    for dst, src in ((rw[:, :], router_w[:, :]), (rb[:, :], router_b.partition_broadcast(P)),
                                     (wq[:, :], Wq[:, :]), (wd[:, :], Wd[:, :]), (wu_raw[0:R, :], Wu[:, :]),
                                     (wu_raw[R:R + 1, :], bu.rearrange("(a n) -> a n", a=1)), (wo[:, :], Wo[:, :]),
                                     (bo_row[:, :], bo.rearrange("(a n) -> a n", a=1)),
                                     (bq_col[:, :], bq.rearrange("(n a) -> n a", a=1)),
                                     (bd_col[:, :], bd.rearrange("(n a) -> n a", a=1))):
                        sp.dma_start(dst, src).then_inc(s_w, 16)
            def load_experts(c):
                e0, e1 = (c % 2) * E // 2, (c % 2 + 1) * E // 2
                if c < 2:
                    sp.dma_start(Wraw[:, c, :].rearrange("p (e f) -> p e f", f=F),
                                 W1[e0:e1, :, :].rearrange("e p f -> p e f")).then_inc(s_wraw[c], 16)
                else:
                    sp.wait_ge(s_split, c - 1)
                    sp.dma_start(Wraw[:, c - 2, :].rearrange("p (g d) -> p g d", d=D),
                                 W2[e0:e1, :, :].rearrange("e (c p) d -> p (e c) d", p=P)).then_inc(s_wraw[c], 16)

            load_experts(0)
            load_experts(1)
            sp.dma_start(b1_all[:, :], b1.rearrange("e f -> (e f)").partition_broadcast(P)).then_inc(s_bias, 16)
            sp.dma_start(b2_all[:, :], b2.rearrange("e f -> (e f)").partition_broadcast(P)).then_inc(s_bias, 16)

            def store_normed(layer):
                def body(u, r, q):
                    wait(sp, norm["r"]["s_xn"], (u + layer * UNITS + 1) * PT)
                    sp.dma_start(xn_dram[bass.ds(u * (PT * P), PT * P), :].rearrange("(t p) d -> p t d", p=P),
                                 norm["r"]["xn"][:, r, :, :]).then_inc(s_xs[r], 16)
                return body

            def load_y(layer):
                def body(u, r, q):
                    wait(sp, s_c1, (u + layer * UNITS - 1) * PT)
                    for c in range(K):
                        sp.dma_start(yb[:, r, c, :, :],
                                     y_dram[bass.ds(u * (PT * P) + c * NTOK, PT * P), :].rearrange("(t p) d -> p t d", p=P)
                                     ).then_inc(s_yl[r], 16)
                return body

            def all_scattered(layer):
                for b in range(YB):
                    wait(sp, s_s[b], 16 * (S // YB) * (layer + 1))

            pipeline(sp, UNITS, 2, [(0, store_normed(0))])
            load_experts(2)
            load_experts(3)
            all_scattered(0)
            pipeline(sp, UNITS, 2, [(0, load_y(0)), (4, store_normed(1))])
            all_scattered(1)

            def store_out(u, r, q):
                wait(sp, s_c1, (u + UNITS + 1) * PT)
                sp.dma_start(out_rows[bass.ds(u * (PT * P), PT * P), :].rearrange("(t p) d -> p t d", p=P),
                             X[:, bass.ds(u * PT, PT), :]).then_inc(s_out, 16)

            pipeline(sp, UNITS, 2, [(0, load_y(1)), (2, store_out)])
            sp.wait_ge(s_out, 16 * UNITS)

        @block.gpsimd
        def _(po):
            G = nc.gpsimd
            G.memset(ident[:, :], 0.0).then_inc(s_cz, 1)
            G.memset(below[:, :], 1.0).then_inc(s_cz, 1)
            G.memset(head_mask[:, :, :], 1.0).then_inc(s_cz, 1)
            G.memset(carry[:, :, :], 1.0).then_inc(s_cz, 1)
            po.wait_ge(s_cz, 4)
            G.affine_select(out=ident[:, :], in_=ident[:, :], compare_op=ALU.not_equal, fill=1.0, base=0,
                            pattern=[[-1, P]], channel_multiplier=1).then_inc(s_const, 1)
            G.affine_select(out=below[:, :], in_=below[:, :], compare_op=ALU.is_gt, fill=0.0, base=0,
                            pattern=[[1, P]], channel_multiplier=-1).then_inc(s_const, 1)
            G.affine_select(out=carry[:, :, :], in_=carry[:, :, :], compare_op=ALU.is_gt, fill=0.0, base=0,
                            pattern=[[0, E], [1, T]], channel_multiplier=0).then_inc(s_const, 1)
            G.affine_select(out=head_mask[:, :, :], in_=head_mask[:, :, :], compare_op=ALU.is_ge, fill=0.0, base=0,
                            pattern=[[-HD, H], [0, HD]], channel_multiplier=1).then_inc(s_cz, 1)
            po.wait_ge(s_cz, 5)
            G.affine_select(out=head_mask[:, :, :], in_=head_mask[:, :, :], compare_op=ALU.is_gt, fill=0.0, base=HD,
                            pattern=[[HD, H], [0, HD]], channel_multiplier=-1).then_inc(s_const, 1)
            G.memset(ones_bf[:, :], 1.0).then_inc(s_const, 1)
            G.memset(ones_e[:, :], 1.0).then_inc(s_const, 1)
            G.memset(ones_row[:, :], 1.0).then_inc(s_const, 1)
            loose = dict(allow_small_or_imprecise_dtypes=True)
            G.iota(iota_lo[:, :], pattern=[[1, P]], base=0, channel_multiplier=0, **loose).then_inc(s_const, 1)
            G.iota(iota_hi[:, :], pattern=[[1, S]], base=0, channel_multiplier=0, **loose).then_inc(s_const, 1)
            G.iota(iota_s[:, :], pattern=[[1, S]], base=0, channel_multiplier=0, **loose).then_inc(s_const, 1)
            G.iota(order[:, :], pattern=[[-1, E]], base=E, channel_multiplier=0, **loose).then_inc(s_const, 1)
            G.iota(steps[:, :], pattern=[[P, THR]], base=0, channel_multiplier=0, **loose).then_inc(s_const, 1)
            G.iota(part[:, :], pattern=[[0, 1]], base=0, channel_multiplier=1, **loose).then_inc(s_const, 1)
            G.iota(dest[:, :, :], pattern=[[1, T], [T, K]], base=-T * K, channel_multiplier=0, **loose).then_inc(s_const, 1)
            G.memset(v1[:, :, :, D:D + 1], 1.0).then_inc(s_fix, 1)

            G.memset(quarter[:, :], 0.25).then_inc(s_fix, 1)
            G.memset(minus_half[:, :], -0.5).then_inc(s_fix, 1)
            po.wait_ge(s_fix, 4)

            def rstd(n, base):
                N = norm[n]

                def body(u, r, q):
                    st, parts = N["st"][:, r, :, :], N["parts"][:, r, :, :]
                    wait(po, N["s_st"], (u + base + 1) * PT)
                    wait(po, N["s_xn"], (u + base - 1) * PT)
                    G.tensor_tensor(parts[:, 0, :], st[:, :, 1], st[:, :, 4], ALU.add)
                    G.tensor_tensor(parts[:, 1, :], st[:, :, 1], st[:, :, 4], ALU.subtract)
                    G.tensor_tensor(parts[:, 2, :], st[:, :, 2], st[:, :, 5], ALU.add).then_inc(N["s_parts"], 1)
                    wait(po, N["s_parts"], u + base + 1)
                    G.tensor_tensor(N["dd"][:, r, :], parts[:, 1, :], parts[:, 1, :], ALU.mult)
                    G.tensor_scalar(N["mean"][:, r, :], parts[:, 0, :], 0.5, None, ALU.mult)
                    G.tensor_scalar(N["vh"][:, r, :], parts[:, 2, :], 1.0 / D, 1e-5, ALU.mult, ALU.add).then_inc(N["s_terms"], 1)
                    wait(po, N["s_terms"], u + base + 1)
                    G.tensor_tensor(N["sq"][:, r, :], N["dd"][:, r, :], quarter[:, :], ALU.mult).then_inc(N["s_sq"], 1)
                    wait(po, N["s_sq"], u + base + 1)
                    G.tensor_tensor(N["ve"][:, r, :], N["sq"][:, r, :], N["vh"][:, r, :], ALU.add).then_inc(N["s_ve"], 1)
                    wait(po, N["s_ve"], u + base + 1)
                    G.tensor_tensor(N["rs"][:, r, :], N["ve"][:, r, :], minus_half[:, :], ALU.pow).then_inc(N["s_rs"], 1)
                return body

            pipeline(po, UNITS, 2, [(0, rstd("r", 0))])

            for c in range(4):
                po.wait_ge(s_wh, c + 1)
                G.tensor_tensor(w_part(W1l, W2l, c), Wraw[:, c % 2, :], w_part(W1h, W2h, c), ALU.subtract).then_inc(s_split, 1)

            for layer in range(2):
                if layer == 1:
                    pipeline(po, UNITS, 2, [(0, rstd("a", 0)), (3, rstd("r", UNITS))])
                po.wait_ge(s_idx, layer + 1)
                for b in range(2):
                    po.wait_ge(s_xs[b], 16 * (UNITS // 2) * (layer + 1))
                for n in range(S + LAG):
                    if n < S:
                        wait(po, s_gT, layer * S + n - GB + 1)
                        G.indirect_dma_start(out=xg[:, n % GB, :], out_offset=None, in_=xn_dram,
                                             in_offset=bass.IndirectOffsetOnAxis(ap=idx_in[:, n:n + 1], axis=0),
                                             bounds_check=NTOK - 1, oob_is_err=False).then_inc(s_g[n % GB], 16)
                    m = n - LAG
                    if m >= 0:
                        po.wait_ge(s_y, layer * S + m + 1)
                        G.indirect_dma_start(out=y_dram, out_offset=bass.IndirectOffsetOnAxis(ap=idx_out[:, m:m + 1], axis=0),
                                             in_=yt[:, m % YB, :], in_offset=None,
                                             bounds_check=K * NTOK - 1, oob_is_err=False).then_inc(s_s[m % YB], 16)

        @block.scalar
        def _(act):
            A_ = nc.scalar

            def copy_xT(n, base):
                N = norm[n]

                def body(u, r, q):
                    wait(act, N["s_tp"], u + base + 1)
                    wait(act, N["s_use"], u + base - 1)
                    A_.activation(N["xT"][:, r, :], bank[0 if n == "r" else 1][:, 0:PT * P], ACT.Copy).then_inc(N["s_xT"], 1)
                return body

            pipeline(act, UNITS, 2, [(0, copy_xT("r", 0))])

            for c in range(4):
                act.wait_ge(s_wraw[c], 16)
                A_.activation(w_part(W1h, W2h, c), Wraw[:, c % 2, :], ACT.Copy).then_inc(s_wh, 1)

            def gates(layer):
                act.wait_ge(s_dm, layer + 1)
                A_.activation(ex[:, :], dm[:, :], ACT.Exp).then_inc(s_ex, 1)

            def experts(layer):
                base = layer * S

                def x_high(n, r, q):
                    wait(act, s_gT, base + n + 1)
                    wait(act, s_up, base + n - 1)
                    A_.activation(xh[:, r % 2, :], bank[r % 2][:, 0:P], ACT.Copy).then_inc(s_xh, 1)

                def h_high(n, r, q):
                    wait(act, s_hT, base + n + 1)
                    wait(act, s_dn, base + n - 1)
                    A_.activation(hh[:, r % 2, :], bank[4 + r % 2][:, :], ACT.Relu).then_inc(s_hh, 1)

                pipeline(act, S, UNROLL, [(0, x_high), (2, h_high)])

            gates(0)
            experts(0)

            def q_c(u, r, q):
                wait(act, s_qc, u + 1)
                wait(act, s_q, u - 1)
                A_.activation(qe[:, r, :], bank[2][:, 0:PT * P], ACT.Exp, bias=bq_col[:, 0:1])
                A_.activation(qr[:, r, :], bank[2][:, 0:PT * P], ACT.Relu, bias=bq_col[:, 0:1]).then_inc(s_qe, 1)
                wait(act, s_kv, u - 1)
                A_.activation(cT[0:R, r, :], bank[2][0:R, PT * P:2 * PT * P], ACT.Identity, bias=bd_col[:, 0:1]).then_inc(s_cT, 1)

            def k_v(u, r, q):
                kv = bank[3][:, :].rearrange("p (t s d) -> p t s d", t=PT, s=2)
                wait(act, s_kv, u + 1)
                wait(act, s_k, u - 1)
                A_.activation(ke[:, r, :, :], kv[:, :, 0, :], ACT.Exp)
                A_.activation(kr[:, r, :, :], kv[:, :, 0, :], ACT.Relu)
                wait(act, s_cp, u - 1)
                A_.activation(v1[:, r, :, 0:D], kv[:, :, 1, :], ACT.Copy).then_inc(s_ke, 1)

            act.wait_ge(s_fix, 4)
            pipeline(act, UNITS, 2, [(0, copy_xT("a", 0)), (0, q_c), (1, k_v), (3, copy_xT("r", UNITS))])
            gates(1)
            experts(1)

        @block.tensor
        def _(pe):
            M = nc.tensor

            def transpose_x(n, base):
                N = norm[n]

                def body(u, r, q):
                    wait(pe, N["s_xn"], (u + base + 1) * PT)
                    wait(pe, N["s_xT"], u + base)
                    for j in range(PT):
                        last = M.transpose(bank[0 if n == "r" else 1][:, j * P:(j + 1) * P], N["xn"][:, r, j, :], ident[:, :])
                    last.then_inc(N["s_tp"], 1)
                return body

            def logits(base):
                def body(u, r, q):
                    wait(pe, norm["r"]["s_xT"], u + base + 1)
                    wait(pe, s_lg, u + base)
                    for j in range(PT):
                        last = M.matmul(bank[7][:, j * E:(j + 1) * E], norm["r"]["xT"][:, r, j * P:(j + 1) * P], rw[:, :],
                                        start=True, stop=True)
                    last.then_inc(s_pl, 1)
                return body

            def slots(layer):
                pe.wait_ge(s_mask, layer + 1)
                m = mask[:, :, :].rearrange("p t e -> p (t e)")
                M.matmul(bank[0][:, 0:T * E], ones_bf[:, :], m, start=True, stop=True)
                M.matmul(bank[1][:, 0:T * E], below[:, :], m, start=True, stop=True).then_inc(s_rank, 1)

                def body(c, r, q):
                    wait(pe, s_oh, layer * T * K + c + 1)
                    M.matmul(bank[2][:, 0:2 * S], A[:, r, :], Hh[:, r, :, :].rearrange("p a s -> p (a s)"),
                             start=False, stop=False, skip_group_check=True).then_inc(s_acc, 1)

                pe.wait_ge(s_oh, layer * T * K + 1)
                M.matmul(bank[2][:, 0:2 * S], A[:, 0, :], Hh[:, 0, :, :].rearrange("p a s -> p (a s)"),
                         start=True, stop=False, skip_group_check=True).then_inc(s_acc, 1)
                for c in range(1, UNROLL):
                    body(c, c, 0)
                with pe.Fori(1, T * K // UNROLL) as i:
                    for j in range(UNROLL):
                        body(i * UNROLL + j, j, i)

            def experts(layer):
                base = layer * S
                pe.wait_ge(s_eid, layer + 1)

                def transpose_gathered(n, r, q):
                    wait(pe, s_g[r % GB], 16 * (q + layer * (S // GB) + 1))
                    wait(pe, s_xl, base + n - 1)
                    M.transpose(bank[r % 2][:, 0:P], xg[:, r % GB, :], ident[:, :]).then_inc(s_gT, 1)

                def up(n, r, q):
                    e = pe.value_load(eid[0:1, bass.ds(n, 1)], min_val=0, max_val=E - 1)
                    o = bank[2 + r % 2][:, :]
                    wait(pe, s_xl, base + n + 1)
                    wait(pe, s_hb, base + n - 1)
                    M.matmul(o, xh[:, r % 2, :], W1h[:, bass.ds(e * F, F)], start=True, stop=False)
                    M.matmul(o, xh[:, r % 2, :], W1l[:, bass.ds(e * F, F)], start=False, stop=False)
                    M.matmul(o, xl[:, r % 2, :], W1h[:, bass.ds(e * F, F)], start=False, stop=True).then_inc(s_up, 1)

                def transpose_hidden(n, r, q):
                    wait(pe, s_hb, base + n + 1)
                    wait(pe, s_hl, base + n - 1)
                    for c in range(FC):
                        last = M.transpose(bank[4 + r % 2][:, c * P:(c + 1) * P], hb[:, r % 2, c * P:(c + 1) * P], ident[:, :])
                    last.then_inc(s_hT, 1)

                def down(n, r, q):
                    e = pe.value_load(eid[0:1, bass.ds(n, 1)], min_val=0, max_val=E - 1)
                    o = bank[6 + r % 2][:, 0:D]
                    wait(pe, s_hl, base + n + 1)
                    wait(pe, s_y, base + n - 1)
                    for c in range(FC):
                        h, l = hh[:, r % 2, c * P:(c + 1) * P], hl[:, r % 2, c * P:(c + 1) * P]
                        M.matmul(o, h, W2h[:, bass.ds(e * F + c * P, D)], start=(c == 0), stop=False)
                        M.matmul(o, h, W2l[:, bass.ds(e * F + c * P, D)], start=False, stop=False)
                        last = M.matmul(o, l, W2h[:, bass.ds(e * F + c * P, D)], start=False, stop=(c == FC - 1))
                    last.then_inc(s_dn, 1)

                pipeline(pe, S, UNROLL, [(0, transpose_gathered), (1, up), (2, transpose_hidden), (3, down)])

            pe.wait_ge(s_const, 14)
            pe.wait_ge(s_w, 160)
            pipeline(pe, UNITS, 2, [(0, transpose_x("r", 0)), (1, logits(0))])
            slots(0)
            pe.wait_ge(s_split, 4)
            experts(0)

            def q_c(u, r, q):
                N = norm["a"]
                wait(pe, N["s_xT"], u + 1)
                wait(pe, s_cT, u)
                M.matmul(bank[2][:, 0:PT * P], wq[:, :], N["xT"][:, r, :], start=True, stop=True)
                M.matmul(bank[2][0:R, PT * P:2 * PT * P], wd[:, :], N["xT"][:, r, :], start=True, stop=True).then_inc(s_qc, 1)

            def k_v(u, r, q):
                wait(pe, s_cT, u + 1)
                wait(pe, s_ke, u)
                for j in range(PT):
                    last = M.matmul(bank[3][:, j * 2 * D:(j + 1) * 2 * D], cT[:, r, j * P:(j + 1) * P],
                                    wu[:, :, :].rearrange("r s d -> r (s d)"), start=True, stop=True)
                last.then_inc(s_kv, 1)

            def context(u, r, q):
                wait(pe, s_k, u + 1)
                wait(pe, s_cx, 2 * u)
                for j in range(PT):
                    last = M.matmul(bank[4][:, 0:D + 1], kk[:, r, j, :], v1[:, r, j, :], start=(j == 0), stop=(j == PT - 1))
                last.then_inc(s_cp, 1)

            def out_z(u, r, q):
                wait(pe, s_q, u + 1)
                wait(pe, s_cx, 2 * (u + 1))
                wait(pe, s_oT, u)
                M.matmul(bank[5][:, 0:PT * P], cx[:, r, :], qT[:, r, :], start=True, stop=True)
                M.matmul(bank[5][:, PT * P:2 * PT * P], ks[:, r, :], qT[:, r, :], start=True, stop=True).then_inc(s_oz, 1)

            def project(u, r, q):
                wait(pe, s_oT, u + 1)
                wait(pe, s_x2, u)
                for j in range(PT):
                    o = bank[6][:, j * D:(j + 1) * D]
                    M.matmul(o, ones_row[:, :], bo_row[:, :], start=True, stop=False)
                    last = M.matmul(o, oT[:, r, j * P:(j + 1) * P], wo[:, :], start=False, stop=True)
                last.then_inc(s_pr, 1)

            pe.wait_ge(s_wu, 1)
            pe.wait_ge(s_fix, 4)
            pipeline(pe, UNITS, 2, [(0, transpose_x("a", 0)), (0, q_c), (1, k_v), (1, context), (2, out_z), (2, project),
                                    (3, transpose_x("r", UNITS)), (4, logits(UNITS))])
            slots(1)
            experts(1)

        @block.vector
        def _(dv):
            V = nc.vector

            def settled():
                dv.wait_ge(s_const, 14)

            def normalise(n, base, ready):
                N = norm[n]

                def body(u, r, q):
                    settled()
                    ready(u)
                    for j in range(PT):
                        V.bn_stats(N["st"][:, r, j, :], X[:, bass.ds(u * PT + j, 1), :].rearrange("p a d -> p (a d)")).then_inc(N["s_st"], 1)
                    wait(dv, N["s_rs"], u + base + 1)
                    wait(dv, N["s_tp"], u + base - 1)
                    if n == "r":
                        wait(dv, s_xs[r], 16 * (q + base // 2))
                    for j in range(PT):
                        V.tensor_scalar(N["xn"][:, r, j, :], X[:, bass.ds(u * PT + j, 1), :].rearrange("p a d -> p (a d)"),
                                        N["mean"][:, r, j:j + 1], N["rs"][:, r, j:j + 1], ALU.subtract, ALU.mult).then_inc(N["s_xn"], 1)
                return body

            def logits(base):
                def body(u, r, q):
                    wait(dv, s_pl, u + base + 1)
                    V.tensor_tensor(LG[:, bass.ds(u * PT, PT), :], bank[7][:, 0:PT * E].rearrange("p (t e) -> p t e", e=E),
                                    rb[:, :].unsqueeze(1).to_broadcast([P, PT, E]), ALU.add).then_inc(s_lg, 1)
                return body

            done = [0]

            def then(ins):
                done[0] += 1
                ins.then_inc(s_rt, 1)
                dv.wait_ge(s_rt, done[0])

            def over_e(a):
                return a.unsqueeze(2).to_broadcast([P, T, E])

            def over_t(a):
                return a.unsqueeze(1).to_broadcast([P, T, E])

            def route(layer):
                lg = LG[:, :, :]
                dv.wait_ge(s_lg, UNITS * (layer + 1))
                then(V.tensor_reduce(m1[:, :], lg, AX.X, ALU.max))
                then(V.tensor_tensor(wa[:, :, :], lg, over_e(m1[:, :]), ALU.is_equal))
                then(V.tensor_tensor(wb[:, :, :], wa[:, :, :], over_t(order[:, :]), ALU.mult))
                then(V.tensor_reduce(r12[:, 0, :], wb[:, :, :], AX.X, ALU.max))
                then(V.tensor_tensor(oh1[:, :, :], over_e(r12[:, 0, :]), over_t(order[:, :]), ALU.is_equal))
                then(V.tensor_scalar(wa[:, :, :], oh1[:, :, :], 0.5, -BIG, ALU.subtract, ALU.mult))
                then(V.tensor_tensor(wb[:, :, :], lg, wa[:, :, :], ALU.min))
                then(V.tensor_reduce(m2[:, :], wb[:, :, :], AX.X, ALU.max))
                V.tensor_tensor(dm[:, :], m2[:, :], m1[:, :], ALU.subtract).then_inc(s_dm, 1)
                then(V.tensor_tensor(wa[:, :, :], wb[:, :, :], over_e(m2[:, :]), ALU.is_equal))
                then(V.tensor_tensor(wc[:, :, :], wa[:, :, :], over_t(order[:, :]), ALU.mult))
                then(V.tensor_reduce(r12[:, 1, :], wc[:, :, :], AX.X, ALU.max))
                then(V.tensor_tensor(oh2[:, :, :], over_e(r12[:, 1, :]), over_t(order[:, :]), ALU.is_equal))
                V.tensor_tensor(mask[:, :, :], oh1[:, :, :], oh2[:, :, :], ALU.add).then_inc(s_mask, 1)
                dv.wait_ge(s_ex, layer + 1)
                then(V.tensor_scalar(den[:, :], ex[:, :], 1.0, None, ALU.add))
                then(V.reciprocal(rden[:, :], den[:, :]))
                then(V.tensor_scalar(gate[:, 0, :], rden[:, :], 0.5, None, ALU.mult))
                then(V.tensor_tensor(gate[:, 1, :], ex[:, :], gate[:, 0, :], ALU.mult))
                dv.wait_ge(s_rank, layer + 1)
                ct = cnt[:, :].rearrange("p (e t) -> p e t", e=E)
                then(V.tensor_copy(ct, bank[0][:, 0:T * E].rearrange("p (t e) -> p e t", e=E)))
                then(V.tensor_tensor_scan(cum[:, :], carry[:, :, :].rearrange("p e t -> p (e t)"), cnt[:, :], 0.0, ALU.mult, ALU.add))
                cu = cum[:, :].rearrange("p (e t) -> p e t", e=E)
                then(V.tensor_tensor(cmp_te[:, :, :], cu[:, :, T - 1:T].to_broadcast([P, E, THR]),
                                     steps[:, :].unsqueeze(1).to_broadcast([P, E, THR]), ALU.is_gt))
                then(V.tensor_reduce(tiles_e[:, :], cmp_te[:, :, :], AX.X, ALU.add))
                then(V.tensor_tensor_scan(tend[:, :], ones_e[:, :], tiles_e[:, :], 0.0, ALU.mult, ALU.add))
                then(V.tensor_tensor(tstart[:, :], tend[:, :], tiles_e[:, :], ALU.subtract))
                then(V.tensor_tensor(wc[:, :, :].rearrange("p t e -> p (t e)"), cum[:, :], cnt[:, :], ALU.subtract))
                before = wc[:, :, :].rearrange("p t e -> p (t e)").rearrange("p (e t) -> p e t", e=E)
                then(V.scalar_tensor_tensor(off[:, :, :], tstart[:, :].unsqueeze(2).to_broadcast([P, E, T]), float(P), before,
                                            ALU.mult, ALU.add))
                then(V.tensor_tensor(pos[:, :, :], bank[1][:, 0:T * E].rearrange("p (t e) -> p t e", e=E),
                                     off[:, :, :].rearrange("p e t -> p t e"), ALU.add))
                for k, oh in enumerate((oh1, oh2)):
                    then(V.tensor_tensor(wa[:, :, :], oh[:, :, :], pos[:, :, :], ALU.mult))
                    then(V.tensor_reduce(slot_f[:, :, k], wa[:, :, :], AX.X, ALU.add))
                then(V.tensor_copy(slot_i[:, :], slot_f[:, :, :].rearrange("p t k -> p (t k)")))
                then(V.tensor_scalar(hi_i[:, :], slot_i[:, :], 7, None, ALU.logical_shift_right))
                then(V.tensor_scalar(lo_i[:, :], slot_i[:, :], P - 1, None, ALU.bitwise_and))
                then(V.tensor_copy(hi_f[:, :], hi_i[:, :]))
                then(V.tensor_copy(lo_f[:, :], lo_i[:, :]))

                def onehots(c, r, q):
                    wait(dv, s_acc, layer * T * K + c - 3)
                    V.tensor_scalar(A[:, r, :], iota_lo[:, :], lo_f[:, bass.ds(c, 1)], None, ALU.is_equal)
                    V.tensor_scalar(Hh[:, r, 0, :], iota_hi[:, :], hi_f[:, bass.ds(c, 1)], part[:, 0:1], ALU.is_equal, ALU.mult)
                    V.tensor_scalar(Hh[:, r, 1, :], iota_hi[:, :], hi_f[:, bass.ds(c, 1)],
                                    dest[:, :, :].rearrange("p t k -> p (t k)")[:, bass.ds(c, 1)], ALU.is_equal, ALU.mult).then_inc(s_oh, 1)

                for c in range(UNROLL):
                    onehots(c, c, 0)
                with dv.Fori(1, T * K // UNROLL) as i:
                    for j in range(UNROLL):
                        onehots(i * UNROLL + j, j, i)
                then(V.tensor_tensor(cmp_s[:, :, :], tend[:, :].unsqueeze(1).to_broadcast([P, S, E]),
                                     iota_s[:, :].unsqueeze(2).to_broadcast([P, S, E]), ALU.is_le))
                then(V.tensor_reduce(eid_f[:, :], cmp_s[:, :, :], AX.X, ALU.add))
                V.tensor_scalar(eid[:, :], eid_f[:, :], float(E - 1), None, ALU.min).then_inc(s_eid, 1)
                dv.wait_ge(s_acc, (layer + 1) * T * K)
                then(V.tensor_scalar(tok_f[:, :], bank[2][:, S:2 * S], float(T * K), float(P), ALU.add, ALU.mult))
                then(V.tensor_tensor(idx_out[:, :], bank[2][:, 0:S], tok_f[:, :], ALU.add))
                V.tensor_scalar(idx_in[:, :], idx_out[:, :], NTOK - 1, None, ALU.bitwise_and).then_inc(s_idx, 1)

            def experts(layer):
                base = layer * S
                dv.wait_ge(s_eid, layer + 1)
                dv.wait_ge(s_bias, 32)

                def x_low(n, r, q):
                    wait(dv, s_xh, base + n + 1)
                    V.tensor_tensor(xl[:, r % 2, :], bank[r % 2][:, 0:P], xh[:, r % 2, :], ALU.subtract).then_inc(s_xl, 1)

                def bias(n, r, q):
                    e = dv.value_load(eid[0:1, bass.ds(n, 1)], min_val=0, max_val=E - 1)
                    wait(dv, s_up, base + n + 1)
                    wait(dv, s_hT, base + n - 1)
                    V.tensor_tensor(hb[:, r % 2, :], bank[2 + r % 2][:, :], b1_all[:, bass.ds(e * F, F)], ALU.add).then_inc(s_hb, 1)

                def h_low(n, r, q):
                    wait(dv, s_hh, base + n + 1)
                    V.scalar_tensor_tensor(hl[:, r % 2, :], bank[4 + r % 2][:, :], 0.0, hh[:, r % 2, :], ALU.max, ALU.subtract).then_inc(s_hl, 1)

                def y(n, r, q):
                    e = dv.value_load(eid[0:1, bass.ds(n, 1)], min_val=0, max_val=E - 1)
                    wait(dv, s_dn, base + n + 1)
                    wait(dv, s_s[r % YB], 16 * (q + layer * (S // YB)))
                    V.tensor_tensor(yt[:, r % YB, :], bank[6 + r % 2][:, 0:D], b2_all[:, bass.ds(e * D, D)], ALU.add).then_inc(s_y, 1)

                pipeline(dv, S, UNROLL, [(0, x_low), (1, bias), (2, h_low), (3, y)])

            def combine(layer):
                def body(u, r, q):
                    wait(dv, s_yl[r], 16 * K * (q + layer * (UNITS // 2) + 1))
                    for k, s in enumerate((s_c0, s_c1)):
                        for j in range(PT):
                            xt = X[:, bass.ds(u * PT + j, 1), :].rearrange("p a d -> p (a d)")
                            V.scalar_tensor_tensor(xt, yb[:, r, k, j, :], gate[:, k, bass.ds(u * PT + j, 1)], xt, ALU.mult, ALU.add).then_inc(s, 1)
                        if k == 0:
                            wait(dv, s, (u + layer * UNITS + 1) * PT)
                return body

            V.memset(cT[R:R + 1, :, :], 1.0).then_inc(s_fix, 1)
            dv.wait_ge(s_const, 14)
            dv.wait_ge(s_w, 160)
            wv = wu_raw[:, :].rearrange("r (h s d) -> r s h d", s=2, d=HD)
            for s in range(2):
                last = V.tensor_copy(wu[:, s, :].rearrange("r (h d) -> r h d", d=HD), wv[:, s, :, :])
            last.then_inc(s_wu, 1)
            dv.wait_ge(s_x, 64)
            pipeline(dv, UNITS, 2, [(0, normalise("r", 0, lambda u: None)), (1, logits(0))])
            route(0)
            experts(0)

            def q_k(u, r, q):
                wait(dv, s_qe, u + 1)
                wait(dv, s_oz, u - 1)
                V.scalar_tensor_tensor(qT[:, r, :], qe[:, r, :], 1.0, qr[:, r, :], ALU.min, ALU.add).then_inc(s_q, 1)
                wait(dv, s_ke, u + 1)
                wait(dv, s_cp, u - 1)
                V.scalar_tensor_tensor(kk[:, r, :, :], ke[:, r, :, :], 1.0, kr[:, r, :, :], ALU.min, ALU.add).then_inc(s_k, 1)

            def context(u, r, q):
                hm = head_mask[:, :, :].rearrange("p h d -> p (h d)")
                wait(dv, s_cp, u + 1)
                wait(dv, s_oz, u - 1)
                V.tensor_tensor(cx[:, r, :], bank[4][:, 0:D], hm, ALU.mult).then_inc(s_cx, 1)
                V.tensor_scalar(ks[:, r, :], hm, bank[4][:, D:D + 1], None, ALU.mult).then_inc(s_cx, 1)

            def out_z(u, r, q):
                wait(dv, s_oz, u + 1)
                wait(dv, s_pr, u - 1)
                V.tensor_scalar(zz[:, r, :], bank[5][:, PT * P:2 * PT * P], 1e-6, None, ALU.add).then_inc(s_zz, 1)
                wait(dv, s_zz, u + 1)
                V.reciprocal(rz[:, r, :], zz[:, r, :]).then_inc(s_rz, 1)
                wait(dv, s_rz, u + 1)
                V.tensor_tensor(oT[:, r, :], bank[5][:, 0:PT * P], rz[:, r, :], ALU.mult).then_inc(s_oT, 1)

            def add_attention(u, r, q):
                xt = X[:, bass.ds(u * PT, PT), :]
                wait(dv, s_pr, u + 1)
                V.tensor_tensor(xt, bank[6][:, 0:PT * D].rearrange("p (t d) -> p t d", d=D), xt, ALU.add).then_inc(s_x2, 1)

            pipeline(dv, UNITS, 2, [(0, combine(0)), (0, normalise("a", 0, lambda u: wait(dv, s_c1, (u + 1) * PT))),
                                    (1, q_k), (1, context), (2, out_z), (2, add_attention),
                                    (3, normalise("r", UNITS, lambda u: wait(dv, s_x2, u + 1))), (4, logits(UNITS))])
            route(1)
            experts(1)
            pipeline(dv, UNITS, 2, [(0, combine(1))])


_INS = ['L0_attn_x', 'L0_attn_Wq', 'L0_attn_bq', 'L0_attn_Wd', 'L0_attn_bd', 'L0_attn_Wu', 'L0_attn_bu', 'L0_attn_Wo',
        'L0_attn_bo', 'L0_ffn_router_w', 'L0_ffn_router_b', 'L0_ffn_W1', 'L0_ffn_b1', 'L0_ffn_W2', 'L0_ffn_b2']


def kernel(**inputs):
    import numpy as _np
    import concourse.bacc as _bacc
    from concourse import mybir as _mybir
    from concourse.bass_utils import run_bass_kernel_spmd as _run

    nc = _bacc.Bacc("TRN2", target_bir_lowering=False, num_devices=1)
    arrays, args = {}, []
    for name in _INS:
        a = _np.ascontiguousarray(inputs[name])
        arrays[f"in_{name}_dram"] = a
        args.append(nc.dram_tensor(f"in_{name}_dram", a.shape, _mybir.dt.from_np(a.dtype), kind="ExternalInput").ap())
    shape = tuple(inputs['L0_attn_x'].shape)
    args.append(nc.dram_tensor("out_0_dram", shape, _mybir.dt.float32, kind="ExternalOutput").ap())
    build_macaron_block(nc, *args)
    r = _run(nc, [arrays], core_ids=[0])
    return r.results[0]["out_0_dram"]
```

```python
import concourse.bass as bass
from concourse import mybir
from contextlib import ExitStack


def build_macaron_block(nc, x, Wq, bq, Wd, bd, Wu, bu, Wo, bo, router_w, router_b, W1, b1, W2, b2, out):
    fp32, f32r, bf16, i32 = mybir.dt.float32, mybir.dt.float32r, mybir.dt.bfloat16, mybir.dt.int32
    ALU, ACT, AX = mybir.AluOpType, mybir.ActivationFunctionType, mybir.AxisListType

    P = 128
    B, TB, D = x.shape
    NTOK = B * TB
    T = NTOK // P
    PT = TB // P
    UNITS = B
    E, F = b1.shape
    K = 2
    FC = F // P
    R = Wd.shape[1]
    HD = 8
    H = D // HD
    UNROLL = 4
    TILES_MOST = (NTOK * K + E * (P - 1)) // P
    S = -(-TILES_MOST // UNROLL) * UNROLL
    THR = NTOK // P
    ROUNDS = T * K // UNROLL
    LAG = 7
    GB = YB = 4
    BIG = 3.0e38
    UP_AT, DOWN_AT = 1, 3

    x_rows = x.rearrange("b t d -> (b t) d")
    out_rows = out.rearrange("b t d -> (b t) d")
    xn_dram = nc.dram_tensor("normed_rows", (NTOK, D), fp32, kind="Internal").ap()
    y_dram = nc.dram_tensor("expert_rows", (K * NTOK, D), fp32, kind="Internal").ap()

    ctx = ExitStack()
    with ctx:
        def sb(name, shape, dt=fp32):
            return ctx.enter_context(nc.sbuf_tensor(name, shape, dt))

        def sem(name):
            return ctx.enter_context(nc.semaphore(name))

        X = sb("X", [P, T, D])
        Wraw = sb("Wraw", [P, 2, E * F // 2])
        W1p, W2p = sb("W1p", [P, E, 2, F], f32r), sb("W2p", [P, E * FC, 2, D], f32r)
        b1_all = sb("b1_all", [P, E * F])
        b2_all = sb("b2_all", [P, E * D])
        rw = sb("rw", [P, E])
        rb = sb("rb", [P, E])
        wq = sb("wq", [P, D])
        wd = sb("wd", [P, R])
        wu_raw = sb("wu_raw", [R + 1, 2 * D])
        wu = sb("wu", [R + 1, 2, D])
        wo = sb("wo", [P, D])
        bo_row = sb("bo_row", [1, D])
        bq_col = sb("bq_col", [P, 1])
        bd_col = sb("bd_col", [R, 1])
        ident = sb("ident", [P, P])
        ones_bf = sb("ones_bf", [P, P], bf16)
        below = sb("below", [P, P], bf16)
        iota_lo = sb("iota_lo", [P, P], bf16)
        iota_hi = sb("iota_hi", [P, S], bf16)
        iota_s = sb("iota_s", [P, S])
        order = sb("order", [P, E])
        steps = sb("steps", [P, THR])
        part = sb("part", [P, 1])
        dest = sb("dest", [P, T, K])
        carry = sb("carry", [P, E, T])
        quarter = sb("quarter", [P, T // 4])
        minus_half = sb("minus_half", [P, T // 4])
        ones_e = sb("ones_e", [P, E])
        head_mask = sb("head_mask", [P, H, HD])
        head_of = sb("head_of", [P, H])
        ones_row = sb("ones_row", [1, P])
        norm = {}
        for n in "ra":
            norm[n] = dict(
                st=sb(f"st_{n}", [P, 2, PT, 6]), parts=sb(f"parts_{n}", [P, 2, 3, PT]),
                mean=sb(f"mean_{n}", [P, 2, PT]), dd=sb(f"dd_{n}", [P, 2, PT]), sq=sb(f"sq_{n}", [P, 2, PT]), vh=sb(f"vh_{n}", [P, 2, PT]),
                ve=sb(f"ve_{n}", [P, 2, PT]), rs=sb(f"rs_{n}", [P, 2, PT]),
                xn=sb(f"xn_{n}", [P, 2, PT, D]), xT=sb(f"xT_{n}", [P, 2, PT * P]),
                s_st=sem(f"stats_{n}"), s_parts=sem(f"stat_parts_{n}"), s_terms=sem(f"stat_terms_{n}"), s_sq=sem(f"stat_square_{n}"), s_ve=sem(f"var_eps_{n}"), s_rs=sem(f"rstd_{n}"), s_xn=sem(f"normed_{n}"),
                s_tp=sem(f"transposed_{n}"), s_xT=sem(f"xT_ready_{n}"))
        st0 = sb("st0", [P, T, 6])
        parts0, dd0, sq0, vh0, ve0 = sb("parts0", [P, 3, T]), sb("dd0", [P, T]), sb("sq0", [P, T]), sb("vh0", [P, T]), sb("ve0", [P, T])
        mean0, rs0 = sb("mean0", [P, T]), sb("rs0", [P, T])
        LG = sb("LG", [P, T, E])
        m1, m2 = sb("m1", [P, T]), sb("m2", [P, T])
        wa, wb, wc = sb("wa", [P, T, E]), sb("wb", [P, T, E]), sb("wc", [P, T, E])
        r12 = sb("r12", [P, 2, T])
        oh1, oh2 = sb("oh1", [P, T, E]), sb("oh2", [P, T, E])
        mask = sb("mask", [P, T, E], bf16)
        dm, ex, den, rden = sb("dm", [P, T]), sb("ex", [P, T]), sb("den", [P, T]), sb("rden", [P, T])
        gate = sb("gate", [P, K, T])
        cnt, cum = sb("cnt", [P, E * T]), sb("cum", [P, E * T])
        cmp_te = sb("cmp_te", [P, E, THR])
        tiles_e, tend, tstart = sb("tiles_e", [P, E]), sb("tend", [P, E]), sb("tstart", [P, E])
        off = sb("off", [P, E, T])
        pos = sb("pos", [P, T, E])
        slot_f = sb("slot_f", [P, T, K])
        slot_i, hi_i, lo_i = sb("slot_i", [P, T * K], i32), sb("hi_i", [P, T * K], i32), sb("lo_i", [P, T * K], i32)
        hi_f, lo_f = sb("hi_f", [P, T * K]), sb("lo_f", [P, T * K])
        cmp_s = sb("cmp_s", [P, S, E])
        eid_f = sb("eid_f", [P, S])
        eid_up, eid_down = sb("eid_up", [P, S + UNROLL], i32), sb("eid_down", [P, S + UNROLL], i32)
        A = sb("A", [P, 2, UNROLL, P], bf16)
        Hh = sb("Hh", [P, 2, UNROLL, S], bf16)
        Hp = sb("Hp", [P, 2, UNROLL, 2, S], bf16)
        tok_f = sb("tok_f", [P, S])
        idx_out, idx_in = sb("idx_out", [P, S], i32), sb("idx_in", [P, S], i32)
        xg = sb("xg", [P, GB, D])
        xh, xl = sb("xh", [P, 2, P], f32r), sb("xl", [P, 2, P], f32r)
        hb = sb("hb", [P, 2, F])
        hh, hl = sb("hh", [P, 2, F], f32r), sb("hl", [P, 2, F], f32r)
        yt = sb("yt", [P, YB, D])
        y_high = sb("y_high", [P, 2, D])
        YL = 4
        yb = Wraw[:, :, :].rearrange("p a n -> p (a n)")[:, 0:YL * K * PT * D].rearrange("p (b k t d) -> p b k t d", b=YL, k=K, t=PT)
        qe, qr, qT = sb("qe", [P, 2, PT * P]), sb("qr", [P, 2, PT * P]), sb("qT", [P, 2, PT * P])
        cT = sb("cT", [R + 1, 2, PT * P])
        ke, kr, kk = sb("ke", [P, 2, PT, D]), sb("kr", [P, 2, PT, D]), sb("kk", [P, 2, PT, D])
        v1 = sb("v1", [P, 2, PT, D + 1])
        cx = sb("cx", [P, 2, D + H])
        zz, rz = sb("zz", [P, 2, PT, H]), sb("rz", [P, 2, PT, H])
        on, oT = sb("on", [P, 2, PT, D]), sb("oT", [P, 2, PT * P])

        bank = [ctx.enter_context(nc.psum_tensor(f"bank{i}", [P, 512], fp32)) for i in range(8)]

        s_x, s_w, s_wraw, s_bias = [sem(f"x_quarter_loaded{c}") for c in range(4)], sem("small_weights"), [sem(f"W_part_loaded{c}") for c in range(4)], sem("biases")
        s_const = sem("constants")
        s_cz = sem("constants_cleared")
        s_wh, s_split = sem("W_high_parts"), sem("W_split")
        s_wu, s_fix = sem("wu_ready"), sem("fixed_ones")
        s_qc = sem("q_c_in_psum")
        s_pl, s_lg = sem("logits_in_psum"), sem("logits")
        norm["r"]["s_use"], norm["a"]["s_use"] = s_pl, s_qc
        s_xs = [sem(f"normed_stored{i}") for i in range(2)]
        s_rt = sem("routing_step")
        s_dm, s_ex = sem("gate_difference"), sem("gate_exp")
        s_mask, s_rank = sem("mask"), sem("ranks")
        s_oh, s_hp, s_hd = sem("slot_onehots"), sem("slot_partitions"), sem("slot_destinations")
        s_st0, s_parts0, s_terms0, s_sq0, s_ve0, s_rs0 = (sem(n) for n in ("stats0", "stat_parts0", "stat_terms0", "stat_square0", "var_eps0", "rstd0"))
        s_acc = sem("onehots_used")
        s_eid, s_idx = sem("expert_ids"), sem("indices")
        s_g = [sem(f"gathered{i}") for i in range(GB)]
        s_s = [sem(f"scattered{i}") for i in range(YB)]
        s_gT, s_xh, s_xl, s_up = sem("gathered_transposed"), sem("x_high"), sem("x_low"), sem("up_done")
        s_hb, s_hT, s_hh, s_hl = sem("hidden_biased"), sem("hidden_transposed"), sem("h_high"), sem("h_low")
        s_dn, s_y = sem("down_done"), sem("y_ready")
        s_yh = sem("y_high_part")
        s_yl = [sem(f"y_loaded{i}") for i in range(YL)]
        s_c0, s_c1 = sem("first_choice_added"), sem("second_choice_added")
        s_qe, s_q, s_cT = sem("q_exp_relu"), sem("q"), sem("c")
        s_kv, s_ke, s_k = sem("k_v_in_psum"), sem("k_exp_relu_v"), sem("k")
        s_cp, s_cx = sem("context_in_psum"), sem("context")
        s_oz, s_zz, s_rz, s_on = sem("out_z_in_psum"), sem("z_plus_eps"), sem("z_reciprocal"), sem("attn_out")
        s_oTp, s_oT = sem("attn_out_transposed"), sem("attn_out_T")
        s_pr, s_x2 = sem("projected"), sem("attn_added")
        s_out = sem("stored")

        def wait(eng, s, value):
            if not (isinstance(value, int) and value <= 0):
                eng.wait_ge(s, value)

        def w_part(c, half):
            if c < 2:
                return W1p[:, c * E // 2:(c + 1) * E // 2, half, :]
            return W2p[:, (c - 2) * E * FC // 2:(c - 1) * E * FC // 2, half, :]

        def w_raw(c):
            return Wraw[:, c % 2, :].rearrange("p (g n) -> p g n", n=F if c < 2 else D)

        def pipeline(eng, count, unroll, stages):
            deepest = max(lag for lag, _ in stages)
            first = -(-(deepest + max(2, unroll)) // unroll) * unroll
            rounds = (count - first) // unroll

            def peeled(s):
                for lag, body in stages:
                    if 0 <= s - lag < count:
                        body(s - lag, (s - lag) % unroll, (s - lag) // unroll)

            for s in range(first):
                peeled(s)
            with eng.Fori(0, rounds) as i:
                for j in range(unroll):
                    for lag, body in stages:
                        n = first + j - lag
                        body(i * unroll + n, n % unroll, i + n // unroll)
            for s in range(first + rounds * unroll, count + deepest):
                peeled(s)

        def tile_pipeline(eng, load_up, load_down, stages):
            def experts_of(table, at, start):
                _, values = nc.values_load_multi_w_load_instructions(
                    table[0:1, start], engines=[eng.engine], min_val=0, max_val=E - 1,
                    skip_runtime_bounds_check_because="the table holds a count of experts, at most E - 1")
                return values

            def peeled(s):
                for lag, body in stages:
                    n = s - lag
                    if 0 <= n < S:
                        e = None
                        if (lag == UP_AT and load_up) or (lag == DOWN_AT and load_down):
                            table = eid_up if lag == UP_AT else eid_down
                            e, = experts_of(table, lag, slice(n + lag, n + lag + 1))
                        body(n, n % UNROLL, n // UNROLL, e)

            first = 2 * UNROLL
            for s in range(first):
                peeled(s)
            with eng.Fori(0, (S - first) // UNROLL) as i:
                ups = experts_of(eid_up, UP_AT, bass.ds(i * UNROLL + first, UNROLL)) if load_up else None
                downs = experts_of(eid_down, DOWN_AT, bass.ds(i * UNROLL + first, UNROLL)) if load_down else None
                for j in range(UNROLL):
                    for lag, body in stages:
                        n = first + j - lag
                        e = ups[j] if lag == UP_AT and load_up else downs[j] if lag == DOWN_AT and load_down else None
                        body(i * UNROLL + n, n % UNROLL, i + n // UNROLL, e)
            for s in range(S, S + max(lag for lag, _ in stages)):
                peeled(s)

        block = ctx.enter_context(nc.Block())

        @block.sync
        def _(sp):
            for c in range(4):
                t0 = c * T // 4
                sp.dma_start(X[:, t0:t0 + T // 4, :], x_rows[t0 * P:(t0 + T // 4) * P, :].rearrange("(t p) d -> p t d", p=P)).then_inc(s_x[c], 16)
                if c == 0:
                    for dst, src in ((rw[:, :], router_w[:, :]), (rb[:, :], router_b.partition_broadcast(P)),
                                     (wq[:, :], Wq[:, :]), (wd[:, :], Wd[:, :]), (wu_raw[0:R, :], Wu[:, :]),
                                     (wu_raw[R:R + 1, :], bu.rearrange("(a n) -> a n", a=1)), (wo[:, :], Wo[:, :]),
                                     (bo_row[:, :], bo.rearrange("(a n) -> a n", a=1)),
                                     (bq_col[:, :], bq.rearrange("(n a) -> n a", a=1)),
                                     (bd_col[:, :], bd.rearrange("(n a) -> n a", a=1))):
                        sp.dma_start(dst, src).then_inc(s_w, 16)
            def load_experts(c):
                e0, e1 = (c % 2) * E // 2, (c % 2 + 1) * E // 2
                if c < 2:
                    sp.dma_start(Wraw[:, c, :].rearrange("p (e f) -> p e f", f=F),
                                 W1[e0:e1, :, :].rearrange("e p f -> p e f")).then_inc(s_wraw[c], 16)
                else:
                    sp.wait_ge(s_split, c - 1)
                    sp.dma_start(Wraw[:, c - 2, :].rearrange("p (g d) -> p g d", d=D),
                                 W2[e0:e1, :, :].rearrange("e (c p) d -> p (e c) d", p=P)).then_inc(s_wraw[c], 16)

            load_experts(0)
            load_experts(1)
            sp.dma_start(b1_all[:, :], b1.rearrange("e f -> (e f)").partition_broadcast(P)).then_inc(s_bias, 16)
            sp.dma_start(b2_all[:, :], b2.rearrange("e f -> (e f)").partition_broadcast(P)).then_inc(s_bias, 16)

            def store_normed(layer):
                def body(u, r, q):
                    wait(sp, norm["r"]["s_xn"], (u + layer * UNITS + 1) * PT)
                    sp.dma_start(xn_dram[bass.ds(u * (PT * P), PT * P), :].rearrange("(t p) d -> p t d", p=P),
                                 norm["r"]["xn"][:, r % 2, :, :]).then_inc(s_xs[r % 2], 16)
                return body

            def load_y(layer):
                def body(u, r, q):
                    wait(sp, s_c1, (u + layer * UNITS - YL + 1) * PT)
                    for c in range(K):
                        sp.dma_start(yb[:, r, c, :, :],
                                     y_dram[bass.ds(u * (PT * P) + c * NTOK, PT * P), :].rearrange("(t p) d -> p t d", p=P)
                                     ).then_inc(s_yl[r], 16)
                return body

            def all_scattered(layer):
                for b in range(YB):
                    wait(sp, s_s[b], 16 * (S // YB) * (layer + 1))

            pipeline(sp, UNITS, 2, [(0, store_normed(0))])
            load_experts(2)
            load_experts(3)
            all_scattered(0)
            pipeline(sp, UNITS, YL, [(0, load_y(0)), (7, store_normed(1))])
            all_scattered(1)

            def store_out(u, r, q):
                wait(sp, s_c1, (u + UNITS + 1) * PT)
                sp.dma_start(out_rows[bass.ds(u * (PT * P), PT * P), :].rearrange("(t p) d -> p t d", p=P),
                             X[:, bass.ds(u * PT, PT), :]).then_inc(s_out, 16)

            pipeline(sp, UNITS, YL, [(0, load_y(1)), (3, store_out)])
            sp.wait_ge(s_out, 16 * UNITS)

        @block.gpsimd
        def _(po):
            G = nc.gpsimd
            G.memset(ident[:, :], 0.0).then_inc(s_cz, 1)
            G.memset(below[:, :], 1.0).then_inc(s_cz, 1)
            G.memset(head_mask[:, :, :], 1.0).then_inc(s_cz, 1)
            G.memset(carry[:, :, :], 1.0).then_inc(s_cz, 1)
            G.memset(head_of[:, :], 1.0).then_inc(s_cz, 1)
            po.wait_ge(s_cz, 5)
            G.affine_select(out=ident[:, :], in_=ident[:, :], compare_op=ALU.not_equal, fill=1.0, base=0,
                            pattern=[[-1, P]], channel_multiplier=1).then_inc(s_const, 1)
            G.affine_select(out=below[:, :], in_=below[:, :], compare_op=ALU.is_gt, fill=0.0, base=0,
                            pattern=[[1, P]], channel_multiplier=-1).then_inc(s_const, 1)
            G.affine_select(out=carry[:, :, :], in_=carry[:, :, :], compare_op=ALU.is_gt, fill=0.0, base=0,
                            pattern=[[0, E], [1, T]], channel_multiplier=0).then_inc(s_const, 1)
            G.affine_select(out=head_mask[:, :, :], in_=head_mask[:, :, :], compare_op=ALU.is_ge, fill=0.0, base=0,
                            pattern=[[-HD, H], [0, HD]], channel_multiplier=1).then_inc(s_cz, 1)
            po.wait_ge(s_cz, 6)
            G.affine_select(out=head_mask[:, :, :], in_=head_mask[:, :, :], compare_op=ALU.is_gt, fill=0.0, base=HD,
                            pattern=[[HD, H], [0, HD]], channel_multiplier=-1).then_inc(s_const, 1)
            G.affine_select(out=head_of[:, :], in_=head_of[:, :], compare_op=ALU.is_ge, fill=0.0, base=0,
                            pattern=[[-HD, H]], channel_multiplier=1).then_inc(s_cz, 1)
            po.wait_ge(s_cz, 7)
            G.affine_select(out=head_of[:, :], in_=head_of[:, :], compare_op=ALU.is_gt, fill=0.0, base=HD,
                            pattern=[[HD, H]], channel_multiplier=-1).then_inc(s_const, 1)
            G.memset(ones_bf[:, :], 1.0).then_inc(s_const, 1)
            G.memset(ones_e[:, :], 1.0).then_inc(s_const, 1)
            G.memset(ones_row[:, :], 1.0).then_inc(s_const, 1)
            loose = dict(allow_small_or_imprecise_dtypes=True)
            G.iota(iota_lo[:, :], pattern=[[1, P]], base=0, channel_multiplier=0, **loose).then_inc(s_const, 1)
            G.iota(iota_hi[:, :], pattern=[[1, S]], base=0, channel_multiplier=0, **loose).then_inc(s_const, 1)
            G.iota(iota_s[:, :], pattern=[[1, S]], base=0, channel_multiplier=0, **loose).then_inc(s_const, 1)
            G.iota(order[:, :], pattern=[[-1, E]], base=E, channel_multiplier=0, **loose).then_inc(s_const, 1)
            G.iota(steps[:, :], pattern=[[P, THR]], base=0, channel_multiplier=0, **loose).then_inc(s_const, 1)
            G.iota(part[:, :], pattern=[[0, 1]], base=0, channel_multiplier=1, **loose).then_inc(s_const, 1)
            G.iota(dest[:, :, :], pattern=[[1, T], [T, K]], base=-T * K, channel_multiplier=0, **loose).then_inc(s_const, 1)
            G.memset(v1[:, :, :, D:D + 1], 1.0).then_inc(s_fix, 1)

            G.memset(quarter[:, :], 0.25).then_inc(s_fix, 1)
            G.memset(minus_half[:, :], -0.5).then_inc(s_fix, 1)
            po.wait_ge(s_fix, 4)

            def rstd(n, base):
                N = norm[n]

                def body(u, r, q):
                    st, parts = N["st"][:, r, :, :], N["parts"][:, r, :, :]
                    wait(po, N["s_st"], (u + base + 1) * PT)
                    wait(po, N["s_xn"], (u + base - 1) * PT)
                    G.tensor_tensor(parts[:, 0, :], st[:, :, 1], st[:, :, 4], ALU.add)
                    G.tensor_tensor(parts[:, 1, :], st[:, :, 1], st[:, :, 4], ALU.subtract)
                    G.tensor_tensor(parts[:, 2, :], st[:, :, 2], st[:, :, 5], ALU.add).then_inc(N["s_parts"], 1)
                    wait(po, N["s_parts"], u + base + 1)
                    G.tensor_tensor(N["dd"][:, r, :], parts[:, 1, :], parts[:, 1, :], ALU.mult)
                    G.tensor_scalar(N["mean"][:, r, :], parts[:, 0, :], 0.5, None, ALU.mult)
                    G.tensor_scalar(N["vh"][:, r, :], parts[:, 2, :], 1.0 / D, 1e-5, ALU.mult, ALU.add).then_inc(N["s_terms"], 1)
                    wait(po, N["s_terms"], u + base + 1)
                    G.tensor_tensor(N["sq"][:, r, :], N["dd"][:, r, :], quarter[:, 0:PT], ALU.mult).then_inc(N["s_sq"], 1)
                    wait(po, N["s_sq"], u + base + 1)
                    G.tensor_tensor(N["ve"][:, r, :], N["sq"][:, r, :], N["vh"][:, r, :], ALU.add).then_inc(N["s_ve"], 1)
                    wait(po, N["s_ve"], u + base + 1)
                    G.tensor_tensor(N["rs"][:, r, :], N["ve"][:, r, :], minus_half[:, 0:PT], ALU.pow).then_inc(N["s_rs"], 1)
                return body

            for c in range(4):
                t = slice(c * T // 4, (c + 1) * T // 4)
                po.wait_ge(s_st0, c + 1)
                G.tensor_tensor(parts0[:, 0, t], st0[:, t, 1], st0[:, t, 4], ALU.add)
                G.tensor_tensor(parts0[:, 1, t], st0[:, t, 1], st0[:, t, 4], ALU.subtract)
                G.tensor_tensor(parts0[:, 2, t], st0[:, t, 2], st0[:, t, 5], ALU.add).then_inc(s_parts0, 1)
                po.wait_ge(s_parts0, c + 1)
                G.tensor_tensor(dd0[:, t], parts0[:, 1, t], parts0[:, 1, t], ALU.mult)
                G.tensor_scalar(mean0[:, t], parts0[:, 0, t], 0.5, None, ALU.mult)
                G.tensor_scalar(vh0[:, t], parts0[:, 2, t], 1.0 / D, 1e-5, ALU.mult, ALU.add).then_inc(s_terms0, 1)
                po.wait_ge(s_terms0, c + 1)
                G.tensor_tensor(sq0[:, t], dd0[:, t], quarter[:, :], ALU.mult).then_inc(s_sq0, 1)
                po.wait_ge(s_sq0, c + 1)
                G.tensor_tensor(ve0[:, t], sq0[:, t], vh0[:, t], ALU.add).then_inc(s_ve0, 1)
                po.wait_ge(s_ve0, c + 1)
                G.tensor_tensor(rs0[:, t], ve0[:, t], minus_half[:, :], ALU.pow).then_inc(s_rs0, 1)

            for c in range(4):
                po.wait_ge(s_wh, c + 1)
                G.tensor_tensor(w_part(c, 1), w_raw(c), w_part(c, 0), ALU.subtract).then_inc(s_split, 1)

            for layer in range(2):
                if layer == 1:
                    pipeline(po, UNITS, 2, [(3, rstd("r", 0)), (0, rstd("a", 0))])
                po.wait_ge(s_idx, layer + 1)
                for b in range(2):
                    po.wait_ge(s_xs[b], 16 * (UNITS // 2) * (layer + 1))
                for n in range(S + LAG):
                    if n < S:
                        wait(po, s_gT, layer * S + n - GB + 1)
                        G.indirect_dma_start(out=xg[:, n % GB, :], out_offset=None, in_=xn_dram,
                                             in_offset=bass.IndirectOffsetOnAxis(ap=idx_in[:, n:n + 1], axis=0),
                                             bounds_check=NTOK - 1, oob_is_err=False).then_inc(s_g[n % GB], 16)
                    m = n - LAG
                    if m >= 0:
                        po.wait_ge(s_y, layer * S + m + 1)
                        G.indirect_dma_start(out=y_dram, out_offset=bass.IndirectOffsetOnAxis(ap=idx_out[:, m:m + 1], axis=0),
                                             in_=yt[:, m % YB, :], in_offset=None,
                                             bounds_check=K * NTOK - 1, oob_is_err=False).then_inc(s_s[m % YB], 16)

        @block.scalar
        def _(act):
            A_ = nc.scalar

            def copy_xT(n, base):
                N = norm[n]

                def body(u, r, q):
                    wait(act, N["s_tp"], u + base + 1)
                    wait(act, N["s_use"], u + base - 1)
                    A_.activation(N["xT"][:, r, :], bank[0 if n == "r" else 1][:, 0:PT * P], ACT.Copy).then_inc(N["s_xT"], 1)
                return body

            pipeline(act, UNITS, 2, [(0, copy_xT("r", 0))])

            for c in range(4):
                act.wait_ge(s_wraw[c], 16)
                A_.activation(w_part(c, 0), w_raw(c), ACT.Copy).then_inc(s_wh, 1)

            def payloads(layer):
                def body(c, r, q):
                    wait(act, s_oh, layer * ROUNDS + c + 1)
                    A_.activation(Hp[:, r, :, 0, :], Hh[:, r, :, :], ACT.Copy, scale=part[:, 0:1]).then_inc(s_hp, 1)
                pipeline(act, ROUNDS, 2, [(0, body)])

            def gates(layer):
                act.wait_ge(s_dm, layer + 1)
                A_.activation(ex[:, :], dm[:, :], ACT.Exp).then_inc(s_ex, 1)

            def experts(layer):
                base = layer * S

                def x_high(n, r, q, e):
                    wait(act, s_gT, base + n + 1)
                    A_.activation(xh[:, r % 2, :], bank[r % 2][:, 0:P], ACT.Copy).then_inc(s_xh, 1)

                def h_high(n, r, q, e):
                    wait(act, s_hT, base + n + 1)
                    A_.activation(hh[:, r % 2, :], bank[4 + r % 2][:, :], ACT.Relu).then_inc(s_hh, 1)

                tile_pipeline(act, False, False, [(0, x_high), (2, h_high)])

            gates(0)
            payloads(0)
            experts(0)

            def q_c(u, r, q):
                wait(act, s_qc, u + 1)
                wait(act, s_q, u - 1)
                A_.activation(qe[:, r, :], bank[2][:, 0:PT * P], ACT.Exp, bias=bq_col[:, 0:1])
                A_.activation(qr[:, r, :], bank[2][:, 0:PT * P], ACT.Relu, bias=bq_col[:, 0:1]).then_inc(s_qe, 1)
                wait(act, s_kv, u - 1)
                A_.activation(cT[0:R, r, :], bank[2][0:R, PT * P:2 * PT * P], ACT.Identity, bias=bd_col[:, 0:1]).then_inc(s_cT, 1)

            def k_v(u, r, q):
                kv = bank[3][:, :].rearrange("p (t s d) -> p t s d", t=PT, s=2)
                wait(act, s_kv, u + 1)
                wait(act, s_k, u - 1)
                A_.activation(ke[:, r, :, :], kv[:, :, 0, :], ACT.Exp)
                A_.activation(kr[:, r, :, :], kv[:, :, 0, :], ACT.Relu)
                wait(act, s_cp, u - 1)
                A_.activation(v1[:, r, :, 0:D], kv[:, :, 1, :], ACT.Copy).then_inc(s_ke, 1)

            def out_T(u, r, q):
                wait(act, s_oTp, u + 1)
                wait(act, s_pr, u - 1)
                A_.activation(oT[:, r, :], bank[6][:, 0:PT * P], ACT.Copy).then_inc(s_oT, 1)

            act.wait_ge(s_fix, 4)
            pipeline(act, UNITS, 2, [(1, q_c), (1, k_v), (2, out_T), (3, copy_xT("r", UNITS)), (0, copy_xT("a", 0))])
            gates(1)
            payloads(1)
            experts(1)

        @block.tensor
        def _(pe):
            M = nc.tensor

            def transpose_x(n, base):
                N = norm[n]

                def body(u, r, q):
                    wait(pe, N["s_xn"], (u + base + 1) * PT)
                    wait(pe, N["s_xT"], u + base)
                    for j in range(PT):
                        last = M.transpose(bank[0 if n == "r" else 1][:, j * P:(j + 1) * P], N["xn"][:, r, j, :], ident[:, :])
                    last.then_inc(N["s_tp"], 1)
                return body

            def logits(base):
                def body(u, r, q):
                    wait(pe, norm["r"]["s_xT"], u + base + 1)
                    wait(pe, s_lg, u + base)
                    for j in range(PT):
                        last = M.matmul(bank[7][:, j * E:(j + 1) * E], norm["r"]["xT"][:, r, j * P:(j + 1) * P], rw[:, :],
                                        start=True, stop=True)
                    last.then_inc(s_pl, 1)
                return body

            def slots(layer):
                pe.wait_ge(s_mask, layer + 1)
                m = mask[:, :, :].rearrange("p t e -> p (t e)")
                M.matmul(bank[0][:, 0:T * E], ones_bf[:, :], m, start=True, stop=True)
                M.matmul(bank[1][:, 0:T * E], below[:, :], m, start=True, stop=True).then_inc(s_rank, 1)

                def body(c, r, q):
                    wait(pe, s_hp, layer * ROUNDS + c + 1)
                    wait(pe, s_hd, layer * ROUNDS + c + 1)
                    for j in range(UNROLL):
                        first = isinstance(c, int) and c == 0 and j == 0
                        final = isinstance(c, int) and c == ROUNDS - 1 and j == UNROLL - 1
                        last = M.matmul(bank[2][:, 0:2 * S], A[:, r, j, :], Hp[:, r, j, :, :].rearrange("p a s -> p (a s)"),
                                        start=first, stop=final, skip_group_check=True)
                    last.then_inc(s_acc, 1)

                pipeline(pe, ROUNDS, 2, [(0, body)])

            def experts(layer):
                base = layer * S
                pe.wait_ge(s_eid, 2 * (layer + 1))

                def transpose_gathered(n, r, q, e):
                    wait(pe, s_g[r % GB], 16 * (q + layer * (S // GB) + 1))
                    M.transpose(bank[r % 2][:, 0:P], xg[:, r % GB, :], ident[:, :]).then_inc(s_gT, 1)

                def up(n, r, q, e):
                    o = bank[2 + r % 2][:, :]
                    w = W1p[:, :, :, :].rearrange("p e a f -> p (e a f)")
                    wait(pe, s_xl, base + n + 1)
                    M.matmul(o, xh[:, r % 2, :], w[:, bass.ds(e * (2 * F), F)], start=True, stop=False)
                    M.matmul(o, xl[:, r % 2, :], w[:, bass.ds(e * (2 * F), F)], start=False, stop=False)
                    M.matmul(o, xh[:, r % 2, :], w[:, bass.ds(e * (2 * F) + F, F)], start=False, stop=True).then_inc(s_up, 1)

                def transpose_hidden(n, r, q, e):
                    wait(pe, s_hb, base + n + 1)
                    for c in range(FC):
                        last = M.transpose(bank[4 + r % 2][:, c * P:(c + 1) * P], hb[:, r % 2, c * P:(c + 1) * P], ident[:, :])
                    last.then_inc(s_hT, 1)

                def down(n, r, q, e):
                    o = bank[6 + r % 2][:, 0:2 * D]
                    w = W2p[:, :, :, :].rearrange("p g a d -> p (g a d)")
                    wait(pe, s_hl, base + n + 1)
                    wait(pe, s_y, base + n - 1)
                    for c in range(FC):
                        wc = w[:, bass.ds(e * (2 * F) + c * 2 * D, 2 * D)]
                        M.matmul(o, hh[:, r % 2, c * P:(c + 1) * P], wc, start=(c == 0), stop=False)
                        last = M.matmul(o, hl[:, r % 2, c * P:(c + 1) * P], wc, start=False, stop=(c == FC - 1))
                    last.then_inc(s_dn, 1)

                tile_pipeline(pe, True, True, [(0, transpose_gathered), (1, up), (2, transpose_hidden), (3, down)])

            pe.wait_ge(s_const, 15)
            pe.wait_ge(s_w, 160)
            pipeline(pe, UNITS, 2, [(0, transpose_x("r", 0)), (1, logits(0))])
            slots(0)
            pe.wait_ge(s_split, 4)
            experts(0)

            def q_c(u, r, q):
                N = norm["a"]
                wait(pe, N["s_xT"], u + 1)
                wait(pe, s_cT, u)
                M.matmul(bank[2][:, 0:PT * P], wq[:, :], N["xT"][:, r, :], start=True, stop=True)
                M.matmul(bank[2][0:R, PT * P:2 * PT * P], wd[:, :], N["xT"][:, r, :], start=True, stop=True).then_inc(s_qc, 1)

            def k_v(u, r, q):
                wait(pe, s_cT, u + 1)
                wait(pe, s_ke, u)
                for j in range(PT):
                    last = M.matmul(bank[3][:, j * 2 * D:(j + 1) * 2 * D], cT[:, r, j * P:(j + 1) * P],
                                    wu[:, :, :].rearrange("r s d -> r (s d)"), start=True, stop=True)
                last.then_inc(s_kv, 1)

            def context(u, r, q):
                wait(pe, s_k, u + 1)
                wait(pe, s_cx, 2 * u)
                for j in range(PT):
                    last = M.matmul(bank[4][:, 0:D + 1], kk[:, r, j, :], v1[:, r, j, :], start=(j == 0), stop=(j == PT - 1))
                last.then_inc(s_cp, 1)

            def out_z(u, r, q):
                wait(pe, s_q, u + 1)
                wait(pe, s_cx, 2 * (u + 1))
                wait(pe, s_on, u)
                for j in range(PT):
                    last = M.matmul(bank[5][:, j * (D + H):(j + 1) * (D + H)], qT[:, r, j * P:(j + 1) * P], cx[:, r, :],
                                    start=True, stop=True)
                last.then_inc(s_oz, 1)

            def transpose_out(u, r, q):
                wait(pe, s_on, u + 1)
                wait(pe, s_x2, u)
                for j in range(PT):
                    last = M.transpose(bank[6][:, j * P:(j + 1) * P], on[:, r, j, :], ident[:, :])
                last.then_inc(s_oTp, 1)

            def project(u, r, q):
                wait(pe, s_oT, u + 1)
                for j in range(PT):
                    o = bank[6][:, PT * P + j * D:PT * P + (j + 1) * D]
                    M.matmul(o, ones_row[:, :], bo_row[:, :], start=True, stop=False)
                    last = M.matmul(o, oT[:, r, j * P:(j + 1) * P], wo[:, :], start=False, stop=True)
                last.then_inc(s_pr, 1)

            pe.wait_ge(s_wu, 1)
            pe.wait_ge(s_fix, 4)
            pipeline(pe, UNITS, 2, [(2, out_z), (1, k_v), (2, transpose_out), (3, transpose_x("r", UNITS)), (2, project),
                                    (1, context), (0, transpose_x("a", 0)), (3, logits(UNITS)), (0, q_c)])
            slots(1)
            experts(1)

        @block.vector
        def _(dv):
            V = nc.vector

            def settled():
                dv.wait_ge(s_const, 15)

            def statistics(n, base):
                N = norm[n]

                def body(u, r, q):
                    settled()
                    if n == "a":
                        wait(dv, s_c1, (u + 1) * PT)
                    else:
                        wait(dv, s_x2, u + 1)
                    for j in range(PT):
                        V.bn_stats(N["st"][:, r, j, :], X[:, bass.ds(u * PT + j, 1), :].rearrange("p a d -> p (a d)")).then_inc(N["s_st"], 1)
                return body

            def normalise(n, base, first=False):
                N = norm[n]

                def body(u, r, q):
                    if not first:
                        wait(dv, N["s_rs"], u + base - UNITS * (n == "r") + 1)
                    wait(dv, N["s_tp"], u + base - 1)
                    if n == "r":
                        wait(dv, s_xs[r], 16 * (q + base // 2))
                    for j in range(PT):
                        t = bass.ds(u * PT + j, 1)
                        mean, rs = (mean0[:, t], rs0[:, t]) if first else (N["mean"][:, r, j:j + 1], N["rs"][:, r, j:j + 1])
                        V.tensor_scalar(N["xn"][:, r, j, :], X[:, t, :].rearrange("p a d -> p (a d)"),
                                        mean, rs, ALU.subtract, ALU.mult).then_inc(N["s_xn"], 1)
                return body

            def logits(base):
                def body(u, r, q):
                    wait(dv, s_pl, u + base + 1)
                    V.tensor_tensor(LG[:, bass.ds(u * PT, PT), :], bank[7][:, 0:PT * E].rearrange("p (t e) -> p t e", e=E),
                                    rb[:, :].unsqueeze(1).to_broadcast([P, PT, E]), ALU.add).then_inc(s_lg, 1)
                return body

            done = [0]

            def then(ins):
                done[0] += 1
                ins.then_inc(s_rt, 1)
                dv.wait_ge(s_rt, done[0])

            def over_e(a):
                return a.unsqueeze(2).to_broadcast([P, T, E])

            def over_t(a):
                return a.unsqueeze(1).to_broadcast([P, T, E])

            def route(layer):
                lg = LG[:, :, :]
                dv.wait_ge(s_lg, UNITS * (layer + 1))
                then(V.tensor_reduce(m1[:, :], lg, AX.X, ALU.max))
                then(V.tensor_tensor(wa[:, :, :], lg, over_e(m1[:, :]), ALU.is_equal))
                then(V.tensor_tensor(wb[:, :, :], wa[:, :, :], over_t(order[:, :]), ALU.mult))
                then(V.tensor_reduce(r12[:, 0, :], wb[:, :, :], AX.X, ALU.max))
                then(V.tensor_tensor(oh1[:, :, :], over_e(r12[:, 0, :]), over_t(order[:, :]), ALU.is_equal))
                then(V.tensor_scalar(wa[:, :, :], oh1[:, :, :], 0.5, -BIG, ALU.subtract, ALU.mult))
                then(V.tensor_tensor(wb[:, :, :], lg, wa[:, :, :], ALU.min))
                then(V.tensor_reduce(m2[:, :], wb[:, :, :], AX.X, ALU.max))
                V.tensor_tensor(dm[:, :], m2[:, :], m1[:, :], ALU.subtract).then_inc(s_dm, 1)
                then(V.tensor_tensor(wa[:, :, :], wb[:, :, :], over_e(m2[:, :]), ALU.is_equal))
                then(V.tensor_tensor(wc[:, :, :], wa[:, :, :], over_t(order[:, :]), ALU.mult))
                then(V.tensor_reduce(r12[:, 1, :], wc[:, :, :], AX.X, ALU.max))
                then(V.tensor_tensor(oh2[:, :, :], over_e(r12[:, 1, :]), over_t(order[:, :]), ALU.is_equal))
                V.tensor_tensor(mask[:, :, :], oh1[:, :, :], oh2[:, :, :], ALU.add).then_inc(s_mask, 1)
                dv.wait_ge(s_ex, layer + 1)
                then(V.tensor_scalar(den[:, :], ex[:, :], 1.0, None, ALU.add))
                then(V.reciprocal(rden[:, :], den[:, :]))
                then(V.tensor_scalar(gate[:, 0, :], rden[:, :], 0.5, None, ALU.mult))
                then(V.tensor_tensor(gate[:, 1, :], ex[:, :], gate[:, 0, :], ALU.mult))
                dv.wait_ge(s_rank, layer + 1)
                ct = cnt[:, :].rearrange("p (e t) -> p e t", e=E)
                then(V.tensor_copy(ct, bank[0][:, 0:T * E].rearrange("p (t e) -> p e t", e=E)))
                then(V.tensor_tensor_scan(cum[:, :], carry[:, :, :].rearrange("p e t -> p (e t)"), cnt[:, :], 0.0, ALU.mult, ALU.add))
                cu = cum[:, :].rearrange("p (e t) -> p e t", e=E)
                then(V.tensor_tensor(cmp_te[:, :, :], cu[:, :, T - 1:T].to_broadcast([P, E, THR]),
                                     steps[:, :].unsqueeze(1).to_broadcast([P, E, THR]), ALU.is_gt))
                then(V.tensor_reduce(tiles_e[:, :], cmp_te[:, :, :], AX.X, ALU.add))
                then(V.tensor_tensor_scan(tend[:, :], ones_e[:, :], tiles_e[:, :], 0.0, ALU.mult, ALU.add))
                then(V.tensor_tensor(tstart[:, :], tend[:, :], tiles_e[:, :], ALU.subtract))
                then(V.tensor_tensor(wc[:, :, :].rearrange("p t e -> p (t e)"), cum[:, :], cnt[:, :], ALU.subtract))
                before = wc[:, :, :].rearrange("p t e -> p (t e)").rearrange("p (e t) -> p e t", e=E)
                then(V.scalar_tensor_tensor(off[:, :, :], tstart[:, :].unsqueeze(2).to_broadcast([P, E, T]), float(P), before,
                                            ALU.mult, ALU.add))
                then(V.tensor_tensor(pos[:, :, :], bank[1][:, 0:T * E].rearrange("p (t e) -> p t e", e=E),
                                     off[:, :, :].rearrange("p e t -> p t e"), ALU.add))
                for k, oh in enumerate((oh1, oh2)):
                    then(V.tensor_tensor(wa[:, :, :], oh[:, :, :], pos[:, :, :], ALU.mult))
                    then(V.tensor_reduce(slot_f[:, :, k], wa[:, :, :], AX.X, ALU.add))
                then(V.tensor_copy(slot_i[:, :], slot_f[:, :, :].rearrange("p t k -> p (t k)")))
                then(V.tensor_scalar(hi_i[:, :], slot_i[:, :], 7, None, ALU.logical_shift_right))
                then(V.tensor_scalar(lo_i[:, :], slot_i[:, :], P - 1, None, ALU.bitwise_and))
                then(V.tensor_copy(hi_f[:, :], hi_i[:, :]))
                then(V.tensor_copy(lo_f[:, :], lo_i[:, :]))

                def onehots(c, r, q):
                    def wide(a, width):
                        return a[:, bass.ds(c * UNROLL, UNROLL)].unsqueeze(2).to_broadcast([P, UNROLL, width])

                    wait(dv, s_acc, layer * ROUNDS + c - 1)
                    V.tensor_tensor(Hh[:, r, :, :], iota_hi[:, :].unsqueeze(1).to_broadcast([P, UNROLL, S]), wide(hi_f, S), ALU.is_equal).then_inc(s_oh, 1)
                    V.tensor_tensor(A[:, r, :, :], iota_lo[:, :].unsqueeze(1).to_broadcast([P, UNROLL, P]), wide(lo_f, P), ALU.is_equal)
                    wait(dv, s_oh, layer * ROUNDS + c + 1)
                    V.tensor_tensor(Hp[:, r, :, 1, :], Hh[:, r, :, :], wide(dest[:, :, :].rearrange("p t k -> p (t k)"), S), ALU.mult).then_inc(s_hd, 1)

                pipeline(dv, ROUNDS, 2, [(0, onehots)])
                then(V.tensor_tensor(cmp_s[:, :, :], tend[:, :].unsqueeze(1).to_broadcast([P, S, E]),
                                     iota_s[:, :].unsqueeze(2).to_broadcast([P, S, E]), ALU.is_le))
                then(V.tensor_reduce(eid_f[:, :], cmp_s[:, :, :], AX.X, ALU.add))
                for table, at in ((eid_up, UP_AT), (eid_down, DOWN_AT)):
                    V.tensor_scalar(table[:, at:at + S], eid_f[:, :], float(E - 1), None, ALU.min).then_inc(s_eid, 1)
                dv.wait_ge(s_acc, (layer + 1) * ROUNDS)
                then(V.tensor_scalar(tok_f[:, :], bank[2][:, S:2 * S], float(T * K), float(P), ALU.add, ALU.mult))
                then(V.tensor_tensor(idx_out[:, :], bank[2][:, 0:S], tok_f[:, :], ALU.add))
                V.tensor_scalar(idx_in[:, :], idx_out[:, :], NTOK - 1, None, ALU.bitwise_and).then_inc(s_idx, 1)

            def experts(layer):
                base = layer * S
                dv.wait_ge(s_eid, 2 * (layer + 1))
                dv.wait_ge(s_bias, 32)

                def x_low(n, r, q, e):
                    wait(dv, s_xh, base + n + 1)
                    V.tensor_tensor(xl[:, r % 2, :], bank[r % 2][:, 0:P], xh[:, r % 2, :], ALU.subtract).then_inc(s_xl, 1)

                def bias(n, r, q, e):
                    wait(dv, s_up, base + n + 1)
                    V.tensor_tensor(hb[:, r % 2, :], bank[2 + r % 2][:, :], b1_all[:, bass.ds(e * F, F)], ALU.add).then_inc(s_hb, 1)

                def h_low(n, r, q, e):
                    wait(dv, s_hh, base + n + 1)
                    V.scalar_tensor_tensor(hl[:, r % 2, :], bank[4 + r % 2][:, :], 0.0, hh[:, r % 2, :], ALU.max, ALU.subtract).then_inc(s_hl, 1)

                def y_first(n, r, q, e):
                    wait(dv, s_dn, base + n + 1)
                    V.tensor_tensor(y_high[:, r % 2, :], bank[6 + r % 2][:, 0:D], b2_all[:, bass.ds(e * D, D)], ALU.add).then_inc(s_yh, 1)

                def y(n, r, q, e):
                    wait(dv, s_yh, base + n + 1)
                    wait(dv, s_s[r % YB], 16 * (q + layer * (S // YB)))
                    V.tensor_tensor(yt[:, r % YB, :], bank[6 + r % 2][:, D:2 * D], y_high[:, r % 2, :], ALU.add).then_inc(s_y, 1)

                tile_pipeline(dv, True, True, [(0, x_low), (UP_AT, bias), (4, y), (2, h_low), (DOWN_AT, y_first)])

            def combine(layer):
                def body(u, r, q):
                    wait(dv, s_yl[r], 16 * K * (q + layer * (UNITS // YL) + 1))
                    for k, s in enumerate((s_c0, s_c1)):
                        for j in range(PT):
                            xt = X[:, bass.ds(u * PT + j, 1), :].rearrange("p a d -> p (a d)")
                            V.scalar_tensor_tensor(xt, yb[:, r, k, j, :], gate[:, k, bass.ds(u * PT + j, 1)], xt, ALU.mult, ALU.add).then_inc(s, 1)
                        if k == 0:
                            wait(dv, s, (u + layer * UNITS + 1) * PT)
                return body

            V.memset(cT[R:R + 1, :, :], 1.0).then_inc(s_fix, 1)
            dv.wait_ge(s_const, 15)
            dv.wait_ge(s_w, 160)
            wv = wu_raw[:, :].rearrange("r (h s d) -> r s h d", s=2, d=HD)
            for s in range(2):
                last = V.tensor_copy(wu[:, s, :].rearrange("r (h d) -> r h d", d=HD), wv[:, s, :, :])
            last.then_inc(s_wu, 1)
            for c in range(4):
                dv.wait_ge(s_x[c], 16)
                for t in range(c * T // 4, (c + 1) * T // 4):
                    last = V.bn_stats(st0[:, t, :], X[:, t, :])
                last.then_inc(s_st0, 1)
            dv.wait_ge(s_rs0, 4)
            pipeline(dv, UNITS, 2, [(0, normalise("r", 0, True)), (1, logits(0))])
            route(0)
            experts(0)

            def q_(u, r, q):
                wait(dv, s_qe, u + 1)
                wait(dv, s_oz, u - 1)
                V.scalar_tensor_tensor(qT[:, r % 2, :], qe[:, r % 2, :], 1.0, qr[:, r % 2, :], ALU.min, ALU.add).then_inc(s_q, 1)

            def k_(u, r, q):
                wait(dv, s_ke, u + 1)
                wait(dv, s_cp, u - 1)
                V.scalar_tensor_tensor(kk[:, r % 2, :, :], ke[:, r % 2, :, :], 1.0, kr[:, r % 2, :, :], ALU.min, ALU.add).then_inc(s_k, 1)

            def context(u, r, q):
                wait(dv, s_cp, u + 1)
                wait(dv, s_oz, u - 1)
                V.tensor_tensor(cx[:, r % 2, 0:D], bank[4][:, 0:D], head_mask[:, :, :].rearrange("p h d -> p (h d)"), ALU.mult).then_inc(s_cx, 1)
                V.tensor_scalar(cx[:, r % 2, D:D + H], head_of[:, :], bank[4][:, D:D + 1], None, ALU.mult).then_inc(s_cx, 1)

            def out_z(u, r, q):
                r = r % 2
                o = bank[5][:, 0:PT * (D + H)].rearrange("p (t n) -> p t n", t=PT)
                wait(dv, s_oz, u + 1)
                V.tensor_scalar(zz[:, r, :, :], o[:, :, D:D + H], 1e-6, None, ALU.add).then_inc(s_zz, 1)
                wait(dv, s_zz, u + 1)
                V.reciprocal(rz[:, r, :, :], zz[:, r, :, :]).then_inc(s_rz, 1)
                wait(dv, s_rz, u + 1)
                wait(dv, s_oTp, u - 1)
                for j in range(PT):
                    last = V.tensor_tensor(on[:, r, j, :].rearrange("p (h e) -> p h e", e=HD), o[:, j, 0:D].rearrange("p (h e) -> p h e", e=HD),
                                           rz[:, r, j, :].unsqueeze(2).to_broadcast([P, H, HD]), ALU.mult)
                last.then_inc(s_on, 1)

            def add_attention(u, r, q):
                xt = X[:, bass.ds(u * PT, PT), :]
                wait(dv, s_pr, u + 1)
                V.tensor_tensor(xt, bank[6][:, PT * P:PT * P + PT * D].rearrange("p (t d) -> p t d", d=D), xt, ALU.add).then_inc(s_x2, 1)

            def with_2(body):
                return lambda u, r, q: body(u, r % 2, q * (YL // 2) + r // 2)

            pipeline(dv, UNITS, YL, [(3, add_attention), (3, with_2(statistics("r", UNITS))), (2, with_2(context)),
                                     (0, combine(0)), (0, with_2(statistics("a", 0))), (1, q_), (2, out_z),
                                     (3, with_2(normalise("r", UNITS))), (1, k_), (0, with_2(normalise("a", 0))), (4, logits(UNITS))])
            route(1)
            experts(1)
            pipeline(dv, UNITS, YL, [(0, combine(1))])


_INS = ['L0_attn_x', 'L0_attn_Wq', 'L0_attn_bq', 'L0_attn_Wd', 'L0_attn_bd', 'L0_attn_Wu', 'L0_attn_bu', 'L0_attn_Wo',
        'L0_attn_bo', 'L0_ffn_router_w', 'L0_ffn_router_b', 'L0_ffn_W1', 'L0_ffn_b1', 'L0_ffn_W2', 'L0_ffn_b2']


def kernel(**inputs):
    import numpy as _np
    import concourse.bacc as _bacc
    from concourse import mybir as _mybir
    from concourse.bass_utils import run_bass_kernel_spmd as _run

    nc = _bacc.Bacc("TRN2", target_bir_lowering=False, num_devices=1)
    arrays, args = {}, []
    for name in _INS:
        a = _np.ascontiguousarray(inputs[name])
        arrays[f"in_{name}_dram"] = a
        args.append(nc.dram_tensor(f"in_{name}_dram", a.shape, _mybir.dt.from_np(a.dtype), kind="ExternalInput").ap())
    shape = tuple(inputs['L0_attn_x'].shape)
    args.append(nc.dram_tensor("out_0_dram", shape, _mybir.dt.float32, kind="ExternalOutput").ap())
    build_macaron_block(nc, *args)
    r = _run(nc, [arrays], core_ids=[0])
    return r.results[0]["out_0_dram"]
```

```python
import concourse.bass as bass
from concourse import mybir
from contextlib import ExitStack


def build_macaron_block(nc, x, Wq, bq, Wd, bd, Wu, bu, Wo, bo, router_w, router_b, W1, b1, W2, b2, out):
    fp32, f32r, bf16, i32 = mybir.dt.float32, mybir.dt.float32r, mybir.dt.bfloat16, mybir.dt.int32
    ALU, ACT, AX = mybir.AluOpType, mybir.ActivationFunctionType, mybir.AxisListType

    P = 128
    B, TB, D = x.shape
    NTOK = B * TB
    T = NTOK // P
    PT = TB // P
    UNITS = B
    E, F = b1.shape
    K = 2
    FC = F // P
    R = Wd.shape[1]
    HD = 8
    H = D // HD
    UNROLL = 4
    TILES_MOST = (NTOK * K + E * (P - 1)) // P
    S = -(-TILES_MOST // (2 * UNROLL)) * 2 * UNROLL
    LAG = 7
    GB = YB = 4
    BIG = 3.0e38
    UP_AT, DOWN_AT = 1, 3
    GT = 4
    OB = 3
    OW = 8
    ROUNDS = T * K // OW
    BEHIND = 5

    x_rows = x.rearrange("b t d -> (b t) d")
    out_rows = out.rearrange("b t d -> (b t) d")
    xn_dram = nc.dram_tensor("normed_rows", (NTOK, D), fp32, kind="Internal").ap()
    y_dram = nc.dram_tensor("expert_rows", (NTOK * K, D), fp32, kind="Internal").ap()

    ctx = ExitStack()
    with ctx:
        def sb(name, shape, dt=fp32):
            return ctx.enter_context(nc.sbuf_tensor(name, shape, dt))

        def sem(name):
            return ctx.enter_context(nc.semaphore(name))

        X = sb("X", [P, T, D])
        W1p, W2p = sb("W1p", [P, E, 2, F], f32r), sb("W2p", [P, E * FC, 2, D], f32r)
        b1_all = sb("b1_all", [P, E * F])
        b2_all = sb("b2_all", [P, E * D])
        rw = sb("rw", [P, E])
        rb = sb("rb", [P, E])
        wq = sb("wq", [P, D])
        wd = sb("wd", [P, R])
        wu_raw = sb("wu_raw", [R + 1, 2 * D])
        wu = sb("wu", [R + 1, 2, D])
        wo = sb("wo", [P, D])
        bo_all = sb("bo_all", [P, D])
        bq_col = sb("bq_col", [P, 1])
        bd_col = sb("bd_col", [R, 1])
        ident = sb("ident", [P, P])
        ones_bf = sb("ones_bf", [P, P], bf16)
        below = sb("below", [P, P], bf16)
        iota_lo = sb("iota_lo", [P, P], bf16)
        iota_hi = sb("iota_hi", [P, S], bf16)
        iota_s = sb("iota_s", [P, S])
        onward = sb("onward", [P, T, E])
        part = sb("part", [P, 1])
        dest = sb("dest", [P, T, K], bf16)
        carry = sb("carry", [P, E, T])
        eps = sb("eps", [P, GT])
        minus_one = sb("minus_one", [P, GT])
        minus_half = sb("minus_half", [P, GT])
        ones_e = sb("ones_e", [P, E])
        heads = sb("heads", [P, D + H])
        head_mask, head_of = heads[:, 0:D].rearrange("p (h d) -> p h d", d=HD), heads[:, D:D + H]
        norm = {}
        for n in "ra":
            norm[n] = dict(
                st=sb(f"st_{n}", [P, 2, PT, 6]), mv=sb(f"mean_var_{n}", [P, 2, PT, 2]), ve=sb(f"ve_{n}", [P, 2, PT]),
                nm=sb(f"minus_mean_{n}", [P, 2, PT]), rs=sb(f"rs_{n}", [P, 2, PT]), shift=sb(f"shift_{n}", [P, 2, PT]),
                xn=sb(f"xn_{n}", [P, 2, PT, D]), xT=sb(f"xT_{n}", [P, 2, PT * P]),
                s_st=sem(f"stats_{n}"), s_mv=sem(f"mean_var_ready_{n}"), s_ve=sem(f"var_eps_{n}"), s_pw=sem(f"rstd_{n}"),
                s_rs=sem(f"rstd_shift_{n}"), s_xn=sem(f"normed_{n}"), s_tp=sem(f"transposed_{n}"), s_xT=sem(f"xT_ready_{n}"))
        GROUPS = T // GT
        st0, mv0 = sb("st0", [P, T, 6]), sb("mean_var0", [P, T, 2])
        ve0, nm0, rs0, shift0 = sb("ve0", [P, T]), sb("minus_mean0", [P, T]), sb("rs0", [P, T]), sb("shift0", [P, T])
        XN0 = sb("XN0", [P, T, D])
        xT0 = sb("xT0", [P, 2, GT * P])
        LG = sb("LG", [P, T, E])
        m1, m2 = sb("m1", [P, T]), sb("m2", [P, T])
        wa, wb, wc = sb("wa", [P, T, E]), sb("wb", [P, T, E]), sb("wc", [P, T, E])
        oh12 = sb("oh12", [P, K, T, E])
        oh1, oh2 = oh12[:, 0, :, :], oh12[:, 1, :, :]
        mask = sb("mask", [P, E, T], bf16)
        dm, ex, den, rden = sb("dm", [P, T]), sb("ex", [P, T]), sb("den", [P, T]), sb("rden", [P, T])
        gate = sb("gate", [P, K, T])
        cum, before, place = sb("cum", [P, E * T]), sb("before", [P, E * T]), sb("place", [P, E, T])
        padded, tiles_i = sb("padded", [P, E], i32), sb("tiles_i", [P, E], i32)
        tend, tstart = sb("tend", [P, E]), sb("tstart", [P, E])
        pos = sb("pos", [P, T, E])
        slot_f = sb("slot_f", [P, K, T])
        slot_i, hi_i, lo_i = sb("slot_i", [P, T * K], i32), sb("hi_i", [P, T * K], i32), sb("lo_i", [P, T * K], i32)
        hi_f, lo_f = sb("hi_f", [P, T * K], bf16), sb("lo_f", [P, T * K], bf16)
        cmp_s = sb("cmp_s", [P, S, E])
        picked = cmp_s[:, 0:K * T, :].rearrange("p (k t) e -> p k t e", k=K)
        eid_f = sb("eid_f", [P, S])
        eid = sb("eid", [P, S + DOWN_AT], i32)
        A = sb("A", [P, OB, OW, P], bf16)
        Hh = sb("Hh", [P, OB, OW, S], bf16)
        Hp = sb("Hp", [P, OB, OW, 2, S], bf16)
        tok_f = sb("tok_f", [P, S])
        idx_part, idx_tile = sb("idx_part", [P, S], i32), sb("idx_tile", [P, S], i32)
        idx_out, idx_in = sb("idx_out", [P, S], i32), sb("idx_in", [P, S], i32)
        xg = sb("xg", [P, GB, D])
        xh, xl = sb("xh", [P, 2, P], f32r), sb("xl", [P, 2, P], f32r)
        hb = sb("hb", [P, 2, F])
        hh, hl = sb("hh", [P, 2, F], f32r), sb("hl", [P, 2, F], f32r)
        yt = sb("yt", [P, YB, D])
        y_high = sb("y_high", [P, 2, D])
        YL = 8
        y_own = sb("y_own", [P, YL // 2, PT, K, D])
        y_more = XN0[:, 0:YL // 2 * PT * K, :].rearrange("p (b t k) d -> p b t k d", t=PT, k=K)
        yb = [y_own[:, i, :, :, :] for i in range(YL // 2)] + [y_more[:, i, :, :, :] for i in range(YL // 2)]
        pairs = XN0[:, :, :].rearrange("p t d -> p (t d)").rearrange("p (n b w) -> p n b w", b=2, w=PT * P)
        qe, qr, qT, oT = (pairs[:, i, :, :] for i in range(4))
        ke, kr, kk, on = (pairs[:, i, :, :].rearrange("p b (t d) -> p b t d", d=D) for i in range(4, 8))
        cT = sb("cT", [R + 1, 2, PT * P])
        v1 = sb("v1", [P, 2, PT, D + H])
        cx = sb("cx", [P, 2, D + H])
        zz, rz = sb("zz", [P, 2, PT, H]), sb("rz", [P, 2, PT, H])
        xb = sb("x_plus_bo", [P, 2, PT, D])

        bank = [ctx.enter_context(nc.psum_tensor(f"bank{i}", [P, 512], fp32)) for i in range(8)]

        s_x, s_w, s_wraw, s_bias = [sem(f"x_group_loaded{g}") for g in range(T // GT)], sem("small_weights"), [sem(f"W_part_loaded{c}") for c in range(4)], sem("biases")
        s_const, s_ident, s_eps = sem("constants"), sem("identity"), sem("normalisation_constants")
        CONSTS = 13
        s_cz = sem("constants_cleared")
        s_wh, s_split = sem("W_high_parts"), [sem("W1_split"), sem("W2_split")]
        s_wu, s_fix = sem("wu_ready"), sem("ones_below_c")
        s_qc = sem("q_c_in_psum")
        s_pl, s_pl0, s_lg = sem("logits_in_psum"), sem("first_logits_in_psum"), sem("logits")
        s_xb = sem("x_plus_bo_ready")
        norm["r"]["s_use"], norm["a"]["s_use"] = s_pl, s_qc
        s_xs0, s_xs = sem("first_normed_stored"), [sem(f"normed_stored{i}") for i in range(2)]
        s_rt = sem("routing_step")
        s_dm, s_ex = sem("gate_difference"), sem("gate_exp")
        s_mask, s_rank = sem("mask"), sem("ranks")
        s_oh, s_hp, s_hd = sem("slot_onehots"), sem("slot_partitions"), sem("slot_destinations")
        s_st0, s_mv0, s_ve0, s_pw0, s_rs0, s_tp0, s_xT0 = (sem(n) for n in (
            "stats0", "mean_var_ready0", "var_eps0", "rstd0", "rstd_shift0", "transposed0", "xT_ready0"))
        s_xn0 = [sem("even_normed0"), sem("odd_normed0")]
        s_oa, s_acc = sem("place_onehots"), sem("onehots_used")
        s_eid, s_idx = sem("expert_ids"), sem("indices")
        s_g = [sem(f"gathered{i}") for i in range(GB)]
        s_s = [sem(f"scattered{i}") for i in range(YB)]
        s_gT, s_xh, s_xl, s_up = sem("gathered_transposed"), sem("x_high"), sem("x_low"), sem("up_done")
        s_hb, s_hT, s_hh, s_hl = sem("hidden_biased"), sem("hidden_transposed"), sem("h_high"), sem("h_low")
        s_dn, s_y = sem("down_done"), sem("y_ready")
        s_yh = sem("y_high_part")
        s_yl = [sem(f"y_loaded{i}") for i in range(YL)]
        s_c0, s_c1 = sem("first_choice_added"), sem("second_choice_added")
        s_qe, s_q, s_cT = sem("q_exp_relu"), sem("q"), sem("c")
        s_kv, s_ke, s_k = sem("k_v_in_psum"), sem("k_exp_relu_v"), sem("k")
        s_cp, s_cx = sem("context_in_psum"), sem("context")
        s_oz, s_zz, s_rz, s_on = sem("out_z_in_psum"), sem("z_plus_eps"), sem("z_reciprocal"), sem("attn_out")
        s_oTp, s_oT = sem("attn_out_transposed"), sem("attn_out_T")
        s_pr, s_x2 = sem("projected"), sem("attn_added")
        s_out = sem("stored")

        def wait(eng, s, value):
            if not (isinstance(value, int) and value <= 0):
                eng.wait_ge(s, value)

        def w_part(c, half):
            if c < 2:
                return W1p[:, c * E // 2:(c + 1) * E // 2, half, :]
            return W2p[:, (c - 2) * E * FC // 2:(c - 1) * E * FC // 2, half, :]

        def w_raw(c):
            return w_part(c, 1).bitcast(fp32)

        def pipeline(eng, count, unroll, buffers, stages):
            deepest = max(lag for lag, _ in stages)
            first = -(-(deepest + 2) // unroll) * unroll
            rounds = (count - first) // unroll

            def peeled(s):
                for lag, body in stages:
                    if 0 <= s - lag < count:
                        body(s - lag, (s - lag) % buffers, (s - lag) // buffers)

            for s in range(first):
                peeled(s)
            with eng.Fori(0, rounds) as i:
                for j in range(unroll):
                    for lag, body in stages:
                        n = first + j - lag
                        body(i * unroll + n, n % buffers, i * (unroll // buffers) + n // buffers)
            for s in range(first + rounds * unroll, count + deepest):
                peeled(s)

        def tile_pipeline(eng, experts, stages):
            def experts_of(start):
                _, values = nc.values_load_multi_w_load_instructions(
                    eid[0:1, start], engines=[eng.engine], min_val=0, max_val=E - 1,
                    skip_runtime_bounds_check_because="the table holds a count of experts, at most E - 1")
                return values

            def peeled(s):
                for lag, body in stages:
                    n = s - lag
                    if 0 <= n < S:
                        e = None
                        if experts and lag in (UP_AT, DOWN_AT):
                            e, = experts_of(slice(n + DOWN_AT, n + DOWN_AT + 1))
                        body(n, n % UNROLL, n // UNROLL, e)

            first = 2 * UNROLL
            for s in range(first):
                peeled(s)
            with eng.Fori(0, (S - first) // first) as i:
                known = {}
                for j in range(first):
                    load = {0: (0, 4), 2: (4, 4), 5: (8, 2)}.get(j) if experts else None
                    if load:
                        for k, e in enumerate(experts_of(bass.ds(i * first + first + load[0], load[1]))):
                            known[load[0] + k - DOWN_AT] = e
                    for lag, body in stages:
                        n = first + j - lag
                        body(i * first + n, n % UNROLL, i * 2 + n // UNROLL, known.get(j - lag) if lag in (UP_AT, DOWN_AT) else None)
            for s in range(S, S + max(lag for lag, _ in stages)):
                peeled(s)

        block = ctx.enter_context(nc.Block())

        @block.sync
        def _(sp):
            for g in range(GROUPS):
                t0 = g * GT
                sp.dma_start(X[:, t0:t0 + GT, :], x_rows[t0 * P:(t0 + GT) * P, :].rearrange("(t p) d -> p t d", p=P)).then_inc(s_x[g], 16)
                if g == 2:
                    for dst, src in ((rw[:, :], router_w[:, :]), (rb[:, :], router_b.partition_broadcast(P)),
                                     (wq[:, :], Wq[:, :]), (wd[:, :], Wd[:, :]), (wu_raw[0:R, :], Wu[:, :]),
                                     (wu_raw[R:R + 1, :], bu.rearrange("(a n) -> a n", a=1)), (wo[:, :], Wo[:, :]),
                                     (bo_all[:, :], bo.partition_broadcast(P)),
                                     (bq_col[:, :], bq.rearrange("(n a) -> n a", a=1)),
                                     (bd_col[:, :], bd.rearrange("(n a) -> n a", a=1))):
                        sp.dma_start(dst, src).then_inc(s_w, 16)
            for c in range(4):
                e0, e1 = (c % 2) * E // 2, (c % 2 + 1) * E // 2
                sp.dma_start(w_raw(c), W1[e0:e1, :, :].rearrange("e p f -> p e f") if c < 2 else
                             W2[e0:e1, :, :].rearrange("e (c p) d -> p (e c) d", p=P)).then_inc(s_wraw[c], 16)
            for g in range(1, GROUPS, 2):
                sp.wait_ge(s_xn0[0], g + 1)
                sp.wait_ge(s_xn0[1], g + 1)
                t0 = (g - 1) * GT
                sp.dma_start(xn_dram[t0 * P:(t0 + 2 * GT) * P, :].rearrange("(t p) d -> p t d", p=P),
                             XN0[:, t0:t0 + 2 * GT, :]).then_inc(s_xs0, 16)
                if g == 3:
                    sp.dma_start(b1_all[:, :], b1.rearrange("e f -> (e f)").partition_broadcast(P)).then_inc(s_bias, 16)
                    sp.dma_start(b2_all[:, :], b2.rearrange("e f -> (e f)").partition_broadcast(P)).then_inc(s_bias, 16)

            def store_normed(u, r, q):
                wait(sp, norm["r"]["s_xn"], u + 1)
                sp.dma_start(xn_dram[bass.ds(u * (PT * P), PT * P), :].rearrange("(t p) d -> p t d", p=P),
                             norm["r"]["xn"][:, r % 2, :, :]).then_inc(s_xs[r % 2], 16)

            def load_y(layer, buffers):
                def body(u, r, q):
                    wait(sp, s_c1, (u + layer * UNITS - buffers + 1) * PT)
                    sp.dma_start(yb[r],
                                 y_dram[bass.ds(u * (PT * K * P), PT * K * P), :].rearrange("(t k p) d -> p t k d", p=P, k=K)
                                 ).then_inc(s_yl[r], 16)
                return body

            def all_scattered(layer):
                for b in range(YB):
                    wait(sp, s_s[b], 16 * (S // YB) * (layer + 1))

            all_scattered(0)
            pipeline(sp, UNITS, 2, 2, [(0, load_y(0, 2)), (9, store_normed)])
            all_scattered(1)

            def store_out(u, r, q):
                wait(sp, s_c1, (u + UNITS + 1) * PT)
                sp.dma_start(out_rows[bass.ds(u * (PT * P), PT * P), :].rearrange("(t p) d -> p t d", p=P),
                             X[:, bass.ds(u * PT, PT), :]).then_inc(s_out, 16)

            pipeline(sp, UNITS, YL, YL, [(0, load_y(1, YL)), (6, store_out)])
            sp.wait_ge(s_out, 16 * UNITS)

        @block.gpsimd
        def _(po):
            G = nc.gpsimd
            G.memset(ident[:, :], 0.0).then_inc(s_cz, 1)
            G.memset(eps[:, :], 1e-5).then_inc(s_eps, 1)
            G.memset(minus_one[:, :], -1.0).then_inc(s_eps, 1)
            G.memset(minus_half[:, :], -0.5).then_inc(s_eps, 1)
            po.wait_ge(s_cz, 1)
            G.affine_select(out=ident[:, :], in_=ident[:, :], compare_op=ALU.not_equal, fill=1.0, base=0,
                            pattern=[[-1, P]], channel_multiplier=1).then_inc(s_ident, 1)
            po.wait_ge(s_eps, 3)

            for g in range(GROUPS):
                t = slice(g * GT, (g + 1) * GT)
                po.wait_ge(s_mv0, g + 1)
                G.tensor_tensor(ve0[:, t], mv0[:, t, 1], eps[:, :], ALU.add).then_inc(s_ve0, 1)
                G.tensor_tensor(nm0[:, t], mv0[:, t, 0], minus_one[:, :], ALU.mult)
                po.wait_ge(s_ve0, g + 1)
                G.tensor_tensor(rs0[:, t], ve0[:, t], minus_half[:, :], ALU.pow).then_inc(s_pw0, 1)
                po.wait_ge(s_pw0, g + 1)
                G.tensor_tensor(shift0[:, t], nm0[:, t], rs0[:, t], ALU.mult).then_inc(s_rs0, 1)

            G.memset(below[:, :], 1.0).then_inc(s_cz, 1)
            G.memset(head_mask, 1.0).then_inc(s_cz, 1)
            G.memset(carry[:, :, :], 1.0).then_inc(s_cz, 1)
            G.memset(head_of, 1.0).then_inc(s_cz, 1)
            G.memset(onward[:, :, :], 1.0).then_inc(s_cz, 1)
            po.wait_ge(s_cz, 6)
            G.affine_select(out=onward[:, :, :], in_=onward[:, :, :], compare_op=ALU.is_gt, fill=0.0, base=0,
                            pattern=[[0, T], [1, E]], channel_multiplier=0).then_inc(s_const, 1)
            G.affine_select(out=below[:, :], in_=below[:, :], compare_op=ALU.is_gt, fill=0.0, base=0,
                            pattern=[[1, P]], channel_multiplier=-1).then_inc(s_const, 1)
            G.affine_select(out=carry[:, :, :], in_=carry[:, :, :], compare_op=ALU.is_gt, fill=0.0, base=0,
                            pattern=[[0, E], [1, T]], channel_multiplier=0).then_inc(s_const, 1)
            G.affine_select(out=head_mask, in_=head_mask, compare_op=ALU.is_ge, fill=0.0, base=0,
                            pattern=[[-HD, H], [0, HD]], channel_multiplier=1).then_inc(s_cz, 1)
            G.affine_select(out=head_of, in_=head_of, compare_op=ALU.is_ge, fill=0.0, base=0,
                            pattern=[[-HD, H]], channel_multiplier=1).then_inc(s_cz, 1)
            po.wait_ge(s_cz, 8)
            G.affine_select(out=head_mask, in_=head_mask, compare_op=ALU.is_gt, fill=0.0, base=HD,
                            pattern=[[HD, H], [0, HD]], channel_multiplier=-1).then_inc(s_const, 1)
            G.affine_select(out=head_of, in_=head_of, compare_op=ALU.is_gt, fill=0.0, base=HD,
                            pattern=[[HD, H]], channel_multiplier=-1).then_inc(s_const, 1)
            G.memset(ones_bf[:, :], 1.0).then_inc(s_const, 1)
            G.memset(ones_e[:, :], 1.0).then_inc(s_const, 1)
            G.memset(v1[:, :, :, D:D + H], 1.0).then_inc(s_const, 1)
            loose = dict(allow_small_or_imprecise_dtypes=True)
            G.iota(iota_lo[:, :], pattern=[[1, P]], base=0, channel_multiplier=0, **loose).then_inc(s_const, 1)
            G.iota(iota_hi[:, :], pattern=[[1, S]], base=0, channel_multiplier=0, **loose).then_inc(s_const, 1)
            G.iota(iota_s[:, :], pattern=[[1, S]], base=0, channel_multiplier=0, **loose).then_inc(s_const, 1)
            G.iota(part[:, :], pattern=[[0, 1]], base=0, channel_multiplier=1, **loose).then_inc(s_const, 1)
            G.iota(dest[:, :, :], pattern=[[K, T], [1, K]], base=-T * K, channel_multiplier=0, **loose).then_inc(s_const, 1)

            def rstd(n):
                N = norm[n]

                def body(u, r, q):
                    mv = N["mv"][:, r, :, :]
                    wait(po, N["s_mv"], u + 1)
                    wait(po, N["s_xn"], u - 1)
                    G.tensor_tensor(N["ve"][:, r, :], mv[:, :, 1], eps[:, 0:PT], ALU.add).then_inc(N["s_ve"], 1)
                    G.tensor_tensor(N["nm"][:, r, :], mv[:, :, 0], minus_one[:, 0:PT], ALU.mult)
                    wait(po, N["s_ve"], u + 1)
                    G.tensor_tensor(N["rs"][:, r, :], N["ve"][:, r, :], minus_half[:, 0:PT], ALU.pow).then_inc(N["s_pw"], 1)
                    wait(po, N["s_pw"], u + 1)
                    G.tensor_tensor(N["shift"][:, r, :], N["nm"][:, r, :], N["rs"][:, r, :], ALU.mult).then_inc(N["s_rs"], 1)
                return body

            def x_plus_bo(u, r, q):
                po.wait_ge(s_const, CONSTS)
                wait(po, s_c1, (u + 1) * PT)
                wait(po, s_x2, u - 1)
                G.tensor_tensor(xb[:, r, :, :], X[:, bass.ds(u * PT, PT), :], bo_all[:, :].unsqueeze(1).to_broadcast([P, PT, D]), ALU.add).then_inc(s_xb, 1)

            for c in (2, 3):
                po.wait_ge(s_wh, c + 1)
                G.tensor_tensor(w_part(c, 1), w_raw(c), w_part(c, 0), ALU.subtract).then_inc(s_split[1], 1)

            def destinations(layer):
                def body(c, r):
                    wait(po, s_oh, layer * ROUNDS + c + 1)
                    G.tensor_tensor(Hp[:, r, :, 1, :], Hh[:, r, :, :],
                                    dest[:, :, :].rearrange("p t k -> p (t k)")[:, c * OW:(c + 1) * OW].unsqueeze(2).to_broadcast([P, OW, S]),
                                    ALU.mult).then_inc(s_hd, 1)
                for c in range(ROUNDS):
                    body(c, c % OB)

            for layer in range(2):
                if layer == 1:
                    po.wait_ge(s_w, 160)
                    pipeline(po, UNITS, 4, 2, [(0, rstd("a")), (5, rstd("r")), (3, x_plus_bo)])
                destinations(layer)
                po.wait_ge(s_idx, layer + 1)
                if layer == 0:
                    po.wait_ge(s_xs0, 16 * GROUPS // 2)
                else:
                    for b in range(2):
                        po.wait_ge(s_xs[b], 16 * (UNITS // 2))
                for n in range(S + LAG):
                    if n < S:
                        wait(po, s_gT, layer * S + n - GB + 1)
                        G.indirect_dma_start(out=xg[:, n % GB, :], out_offset=None, in_=xn_dram,
                                             in_offset=bass.IndirectOffsetOnAxis(ap=idx_in[:, n:n + 1], axis=0),
                                             bounds_check=NTOK - 1, oob_is_err=False).then_inc(s_g[n % GB], 16)
                    m = n - LAG
                    if m >= 0:
                        po.wait_ge(s_y, layer * S + m + 1)
                        G.indirect_dma_start(out=y_dram, out_offset=bass.IndirectOffsetOnAxis(ap=idx_out[:, m:m + 1], axis=0),
                                             in_=yt[:, m % YB, :], in_offset=None,
                                             bounds_check=K * NTOK - 1, oob_is_err=False).then_inc(s_s[m % YB], 16)

        @block.scalar
        def _(act):
            A_ = nc.scalar

            def copy_xT(n):
                N = norm[n]

                def body(u, r, q):
                    wait(act, N["s_tp"], u + 1)
                    wait(act, N["s_use"], u - 1)
                    A_.activation(N["xT"][:, r, :], bank[0][:, 0:PT * P], ACT.Copy).then_inc(N["s_xT"], 1)
                return body

            def normalise(n):
                N = norm[n]

                def body(u, r, q):
                    act.wait_ge(s_const, CONSTS)
                    wait(act, N["s_rs"], u + 1)
                    wait(act, N["s_tp"], u - 1)
                    if n == "r":
                        wait(act, s_xs[r], 16 * q)
                    for j in range(PT):
                        last = A_.activation(N["xn"][:, r, j, :], X[:, bass.ds(u * PT + j, 1), :].rearrange("p a d -> p (a d)"),
                                             ACT.Identity, scale=N["rs"][:, r, j:j + 1], bias=N["shift"][:, r, j:j + 1])
                    last.then_inc(N["s_xn"], 1)
                return body

            def first_copy_xT(g):
                act.wait_ge(s_tp0, g + 1)
                if g >= 2:
                    act.wait_ge(s_pl0, g - 1)
                A_.activation(xT0[:, g % 2, :], bank[g % 2][:, :], ACT.Copy).then_inc(s_xT0, 1)

            def w_high(c):
                act.wait_ge(s_wraw[c], 16)
                A_.activation(w_part(c, 0), w_raw(c), ACT.Copy).then_inc(s_wh, 1)

            for g in range(GROUPS + 1):
                if g < GROUPS:
                    act.wait_ge(s_rs0, g + 1)
                    for t in range(g * GT, (g + 1) * GT, 2):
                        last = A_.activation(XN0[:, t, :], X[:, t, :], ACT.Identity, scale=rs0[:, t:t + 1], bias=shift0[:, t:t + 1])
                    last.then_inc(s_xn0[0], 1)
                if g > 0:
                    first_copy_xT(g - 1)
                if g in (5, 7):
                    w_high((g - 5) // 2)
            w_high(2)
            w_high(3)

            def payloads(layer):
                def body(c, r):
                    wait(act, s_oh, layer * ROUNDS + c + 1)
                    A_.activation(Hp[:, r, :, 0, :], Hh[:, r, :, :], ACT.Copy, scale=part[:, 0:1]).then_inc(s_hp, 1)
                for c in range(ROUNDS):
                    body(c, c % OB)

            def gates(layer):
                act.wait_ge(s_dm, layer + 1)
                A_.activation(ex[:, :], dm[:, :], ACT.Exp).then_inc(s_ex, 1)

            def experts(layer):
                base = layer * S

                def x_high(n, r, q, e):
                    wait(act, s_gT, base + n + 1)
                    A_.activation(xh[:, r % 2, :], bank[r % 2][:, 0:P], ACT.Copy).then_inc(s_xh, 1)

                def h_high(n, r, q, e):
                    wait(act, s_hT, base + n + 1)
                    A_.activation(hh[:, r % 2, :], bank[4 + r % 2][:, :], ACT.Relu).then_inc(s_hh, 1)

                tile_pipeline(act, False, [(0, x_high), (2, h_high)])

            gates(0)
            payloads(0)
            experts(0)

            def q_parts(u, r, q):
                wait(act, s_qc, u + 1)
                wait(act, s_q, u - 1)
                A_.activation(qe[:, r, :], bank[2][:, 0:PT * P], ACT.Exp, bias=bq_col[:, 0:1])
                A_.activation(qr[:, r, :], bank[2][:, 0:PT * P], ACT.Relu, bias=bq_col[:, 0:1]).then_inc(s_qe, 1)

            def copy_c(u, r, q):
                wait(act, s_qc, u + 1)
                wait(act, s_kv, u - 1)
                A_.activation(cT[0:R, r, :], bank[2][0:R, PT * P:2 * PT * P], ACT.Identity, bias=bd_col[:, 0:1]).then_inc(s_cT, 1)

            def k_v(u, r, q):
                kv = bank[3][:, :].rearrange("p (t s d) -> p t s d", t=PT, s=2)
                wait(act, s_kv, u + 1)
                wait(act, s_k, u - 1)
                A_.activation(ke[:, r, :, :], kv[:, :, 0, :], ACT.Exp)
                A_.activation(kr[:, r, :, :], kv[:, :, 0, :], ACT.Relu)
                wait(act, s_cp, u - 1)
                A_.activation(v1[:, r, :, 0:D], kv[:, :, 1, :], ACT.Copy).then_inc(s_ke, 1)

            def out_T(u, r, q):
                wait(act, s_oTp, u + 1)
                wait(act, s_pr, u - 1)
                A_.activation(oT[:, r, :], bank[6][:, 0:PT * P], ACT.Copy).then_inc(s_oT, 1)

            act.wait_ge(s_fix, 1)
            pipeline(act, UNITS, 4, 2, [(6, normalise("r")), (2, k_v), (0, normalise("a")), (1, copy_c),
                                        (6, copy_xT("r")), (1, q_parts), (3, out_T), (0, copy_xT("a"))])
            gates(1)
            payloads(1)
            experts(1)

        @block.tensor
        def _(pe):
            M = nc.tensor

            def transpose_x(n):
                N = norm[n]

                def body(u, r, q):
                    wait(pe, N["s_xn"], u + 1)
                    if n == "a":
                        wait(pe, norm["r"]["s_xT"], u - BEHIND)
                    else:
                        wait(pe, norm["a"]["s_xT"], min(u + BEHIND + 1, UNITS) if isinstance(u, int) else u + BEHIND + 1)
                    for j in range(PT):
                        last = M.transpose(bank[0][:, j * P:(j + 1) * P], N["xn"][:, r, j, :], ident[:, :])
                    last.then_inc(N["s_tp"], 1)
                return body

            def logits(u, r, q):
                wait(pe, norm["r"]["s_xT"], u + 1)
                for j in range(PT):
                    last = M.matmul(bank[7][:, bass.ds(u * (PT * E) + j * E, E)], norm["r"]["xT"][:, r, j * P:(j + 1) * P], rw[:, :],
                                    start=True, stop=True)
                last.then_inc(s_pl, 1)

            def first_logits(g):
                pe.wait_ge(s_xT0, g + 1)
                for t in range(g * GT, (g + 1) * GT):
                    last = M.matmul(bank[7][:, t * E:(t + 1) * E], xT0[:, g % 2, (t % GT) * P:(t % GT + 1) * P], rw[:, :],
                                    start=True, stop=True)
                last.then_inc(s_pl0, 1)

            def slots(layer):
                pe.wait_ge(s_mask, layer + 1)
                m = mask[:, :, :].rearrange("p e t -> p (e t)")
                M.matmul(bank[0][:, 0:E * T], ones_bf[:, :], m, start=True, stop=True)
                M.matmul(bank[1][:, 0:E * T], below[:, :], m, start=True, stop=True).then_inc(s_rank, 1)

                def body(c, r):
                    wait(pe, s_hp, layer * ROUNDS + c + 1)
                    wait(pe, s_hd, layer * ROUNDS + c + 1)
                    wait(pe, s_oa, layer * ROUNDS + c + 1)
                    for j in range(OW):
                        first = c == 0 and j == 0
                        final = c == ROUNDS - 1 and j == OW - 1
                        last = M.matmul(bank[2][:, 0:2 * S], A[:, r, j, :], Hp[:, r, j, :, :].rearrange("p a s -> p (a s)"),
                                        start=first, stop=final, skip_group_check=True)
                    last.then_inc(s_acc, 1)

                for c in range(ROUNDS):
                    body(c, c % OB)

            def experts(layer):
                base = layer * S
                pe.wait_ge(s_eid, layer + 1)

                def transpose_gathered(n, r, q, e):
                    wait(pe, s_g[r % GB], 16 * (q + layer * (S // GB) + 1))
                    M.transpose(bank[r % 2][:, 0:P], xg[:, r % GB, :], ident[:, :]).then_inc(s_gT, 1)

                def up(n, r, q, e):
                    o = bank[2 + r % 2][:, :]
                    w = W1p[:, :, :, :].rearrange("p e a f -> p (e a f)")
                    wait(pe, s_xl, base + n + 1)
                    M.matmul(o, xh[:, r % 2, :], w[:, bass.ds(e * (2 * F), F)], start=True, stop=False)
                    M.matmul(o, xl[:, r % 2, :], w[:, bass.ds(e * (2 * F), F)], start=False, stop=False)
                    M.matmul(o, xh[:, r % 2, :], w[:, bass.ds(e * (2 * F) + F, F)], start=False, stop=True).then_inc(s_up, 1)

                def transpose_hidden(n, r, q, e):
                    wait(pe, s_hb, base + n + 1)
                    for c in range(FC):
                        last = M.transpose(bank[4 + r % 2][:, c * P:(c + 1) * P], hb[:, r % 2, c * P:(c + 1) * P], ident[:, :])
                    last.then_inc(s_hT, 1)

                def down(n, r, q, e):
                    o = bank[6 + r % 2][:, 0:2 * D]
                    w = W2p[:, :, :, :].rearrange("p g a d -> p (g a d)")
                    wait(pe, s_hl, base + n + 1)
                    wait(pe, s_y, base + n - 1)
                    for c in range(FC):
                        wc = w[:, bass.ds(e * (2 * F) + c * 2 * D, 2 * D)]
                        M.matmul(o, hh[:, r % 2, c * P:(c + 1) * P], wc, start=(c == 0), stop=False)
                        last = M.matmul(o, hl[:, r % 2, c * P:(c + 1) * P], wc, start=False, stop=(c == FC - 1))
                    last.then_inc(s_dn, 1)

                tile_pipeline(pe, True, [(0, transpose_gathered), (1, up), (2, transpose_hidden), (3, down)])

            pe.wait_ge(s_ident, 1)
            for g in range(GROUPS):
                pe.wait_ge(s_xn0[0], g + 1)
                pe.wait_ge(s_xn0[1], g + 1)
                if g >= 2:
                    pe.wait_ge(s_xT0, g - 1)
                for t in range(g * GT, (g + 1) * GT):
                    last = M.transpose(bank[g % 2][:, (t % GT) * P:(t % GT + 1) * P], XN0[:, t, :], ident[:, :])
                last.then_inc(s_tp0, 1)
                if g == 1:
                    pe.wait_ge(s_w, 160)
                if g > 0:
                    first_logits(g - 1)
            first_logits(GROUPS - 1)
            pe.wait_ge(s_const, CONSTS)
            slots(0)
            for s in s_split:
                pe.wait_ge(s, 2)
            experts(0)

            def q_c(u, r, q):
                N = norm["a"]
                wait(pe, N["s_xT"], u + 1)
                wait(pe, s_cT, u)
                wait(pe, s_qe, u)
                M.matmul(bank[2][:, 0:PT * P], wq[:, :], N["xT"][:, r, :], start=True, stop=True)
                M.matmul(bank[2][0:R, PT * P:2 * PT * P], wd[:, :], N["xT"][:, r, :], start=True, stop=True).then_inc(s_qc, 1)

            def k_v(u, r, q):
                wait(pe, s_cT, u + 1)
                wait(pe, s_ke, u)
                for j in range(PT):
                    last = M.matmul(bank[3][:, j * 2 * D:(j + 1) * 2 * D], cT[:, r, j * P:(j + 1) * P],
                                    wu[:, :, :].rearrange("r s d -> r (s d)"), start=True, stop=True)
                last.then_inc(s_kv, 1)

            def context(u, r, q):
                wait(pe, s_k, u + 1)
                wait(pe, s_cx, u)
                for j in range(PT):
                    last = M.matmul(bank[4][:, 0:D + H], kk[:, r, j, :], v1[:, r, j, :], start=(j == 0), stop=(j == PT - 1))
                last.then_inc(s_cp, 1)

            def out_z(u, r, q):
                wait(pe, s_q, u + 1)
                wait(pe, s_cx, u + 1)
                wait(pe, s_on, u)
                for j in range(PT):
                    last = M.matmul(bank[5][:, j * (D + H):(j + 1) * (D + H)], qT[:, r, j * P:(j + 1) * P], cx[:, r, :],
                                    start=True, stop=True)
                last.then_inc(s_oz, 1)

            def transpose_out(u, r, q):
                wait(pe, s_on, u + 1)
                wait(pe, s_oT, u)
                for j in range(PT):
                    last = M.transpose(bank[6][:, j * P:(j + 1) * P], on[:, r, j, :], ident[:, :])
                last.then_inc(s_oTp, 1)

            def project(u, r, q):
                wait(pe, s_oT, u + 1)
                wait(pe, s_x2, u)
                for j in range(PT):
                    last = M.matmul(bank[1][:, j * D:(j + 1) * D], oT[:, r, j * P:(j + 1) * P], wo[:, :],
                                    start=True, stop=True)
                last.then_inc(s_pr, 1)

            pe.wait_ge(s_wu, 1)
            pe.wait_ge(s_fix, 1)
            pe.wait_ge(s_lg, 1)
            pipeline(pe, UNITS, 4, 2, [(3, transpose_out), (0, transpose_x("a")), (1, k_v), (2, out_z), (0, q_c),
                                       (3, project), (5, transpose_x("r")), (6, logits), (1, context)])
            slots(1)
            experts(1)

        @block.vector
        def _(dv):
            V = nc.vector

            def settled():
                dv.wait_ge(s_const, CONSTS)

            def statistics(n):
                N = norm[n]

                def body(u, r, q):
                    settled()
                    if n == "a":
                        wait(dv, s_c1, (u + 1) * PT)
                    else:
                        wait(dv, s_x2, u + 1)
                    for j in range(PT):
                        last = V.bn_stats(N["st"][:, r, j, :], X[:, bass.ds(u * PT + j, 1), :].rearrange("p a d -> p (a d)"))
                    last.then_inc(N["s_st"], 1)
                return body

            def await_statistics(n):
                def body(u, r, q):
                    wait(dv, norm[n]["s_st"], u + 1)
                return body

            def aggregate(n):
                N = norm[n]

                def body(u, r, q):
                    for j in range(PT):
                        last = V.bn_aggr(N["mv"][:, r, j, :], N["st"][:, r, j, :])
                    last.then_inc(N["s_mv"], 1)
                return body

            done = [0]

            def then(ins):
                done[0] += 1
                ins.then_inc(s_rt, 1)
                dv.wait_ge(s_rt, done[0])

            def over_e(a):
                return a.unsqueeze(2).to_broadcast([P, T, E])

            def over_t(a):
                return a.unsqueeze(1).to_broadcast([P, T, E])

            def route(layer):
                lg = LG[:, :, :]
                if layer == 0:
                    dv.wait_ge(s_pl0, GROUPS)
                else:
                    dv.wait_ge(s_pl, UNITS)
                V.tensor_tensor(lg, bank[7][:, 0:T * E].rearrange("p (t e) -> p t e", e=E), over_t(rb[:, :]), ALU.add).then_inc(s_lg, 1)
                dv.wait_ge(s_lg, layer + 1)
                def flat(a):
                    return a.rearrange("p t e -> p (t e)")

                def first_of(oh, hits):
                    then(V.tensor_tensor_scan(flat(wc[:, :, :]), flat(onward[:, :, :]), flat(hits), 0.0, ALU.mult, ALU.add))
                    return V.scalar_tensor_tensor(oh, wc[:, :, :], 1.0, hits, ALU.is_equal, ALU.mult)

                then(V.tensor_reduce(m1[:, :], lg, AX.X, ALU.max))
                then(V.tensor_tensor(wa[:, :, :], lg, over_e(m1[:, :]), ALU.is_equal))
                then(first_of(oh1, wa[:, :, :]))
                then(V.scalar_tensor_tensor(wb[:, :, :], oh1, -BIG, lg, ALU.mult, ALU.add))
                then(V.tensor_reduce(m2[:, :], wb[:, :, :], AX.X, ALU.max))
                V.tensor_tensor(dm[:, :], m2[:, :], m1[:, :], ALU.subtract).then_inc(s_dm, 1)
                then(V.tensor_tensor(wa[:, :, :], wb[:, :, :], over_e(m2[:, :]), ALU.is_equal))
                then(first_of(oh2, wa[:, :, :]))
                V.tensor_tensor(mask[:, :, :].rearrange("p e t -> p t e"), oh1[:, :, :], oh2[:, :, :], ALU.add).then_inc(s_mask, 1)
                dv.wait_ge(s_rank, layer + 1)
                here = bank[0][:, 0:E * T]
                then(V.tensor_tensor_scan(cum[:, :], carry[:, :, :].rearrange("p e t -> p (e t)"), here, 0.0, ALU.mult, ALU.add))
                V.tensor_scalar(padded[:, :], cum[:, :].rearrange("p (e t) -> p e t", e=E)[:, :, T - 1], float(P - 1), None, ALU.add)
                then(V.tensor_tensor(before[:, :], cum[:, :], here, ALU.subtract))
                V.tensor_scalar(tiles_i[:, :], padded[:, :], 7, None, ALU.logical_shift_right)
                then(V.tensor_tensor(place[:, :, :].rearrange("p e t -> p (e t)"), bank[1][:, 0:E * T], before[:, :], ALU.add))
                then(V.tensor_tensor_scan(tend[:, :], ones_e[:, :], tiles_i[:, :], 0.0, ALU.mult, ALU.add))
                then(V.tensor_tensor(tstart[:, :], tend[:, :], tiles_i[:, :], ALU.subtract))
                then(V.scalar_tensor_tensor(pos[:, :, :].rearrange("p t e -> p e t"), tstart[:, :].unsqueeze(2).to_broadcast([P, E, T]), float(P),
                                            place[:, :, :], ALU.mult, ALU.add))
                then(V.tensor_tensor(picked[:, :, :, :], oh12[:, :, :, :], pos[:, :, :].unsqueeze(1).to_broadcast([P, K, T, E]), ALU.mult))
                then(V.tensor_reduce(slot_f[:, :, :], picked[:, :, :, :], AX.X, ALU.add))
                then(V.tensor_copy(slot_i[:, :].rearrange("p (t k) -> p k t", k=K), slot_f[:, :, :]))
                V.tensor_scalar(hi_i[:, :], slot_i[:, :], 7, None, ALU.logical_shift_right)
                then(V.tensor_scalar(lo_i[:, :], slot_i[:, :], P - 1, None, ALU.bitwise_and))
                V.tensor_copy(hi_f[:, :], hi_i[:, :])
                then(V.tensor_copy(lo_f[:, :], lo_i[:, :]))

                def onehots(c, r):
                    def wide(a, width):
                        return a[:, c * OW:(c + 1) * OW].unsqueeze(2).to_broadcast([P, OW, width])

                    wait(dv, s_acc, layer * ROUNDS + c - OB + 1)
                    V.tensor_tensor(Hh[:, r, :, :], iota_hi[:, :].unsqueeze(1).to_broadcast([P, OW, S]), wide(hi_f, S), ALU.is_equal).then_inc(s_oh, 1)
                    V.tensor_tensor(A[:, r, :, :], iota_lo[:, :].unsqueeze(1).to_broadcast([P, OW, P]), wide(lo_f, P), ALU.is_equal).then_inc(s_oa, 1)

                for c in range(ROUNDS):
                    onehots(c, c % OB)
                then(V.tensor_tensor(cmp_s[:, :, :], tend[:, :].unsqueeze(1).to_broadcast([P, S, E]),
                                     iota_s[:, :].unsqueeze(2).to_broadcast([P, S, E]), ALU.is_le))
                then(V.tensor_reduce(eid_f[:, :], cmp_s[:, :, :], AX.X, ALU.add))
                V.tensor_scalar(eid[:, DOWN_AT:DOWN_AT + S], eid_f[:, :], float(E - 1), None, ALU.min).then_inc(s_eid, 1)
                dv.wait_ge(s_acc, (layer + 1) * ROUNDS)
                then(V.tensor_scalar(tok_f[:, :], bank[2][:, S:2 * S], float(T * K), float(P), ALU.add, ALU.mult))
                then(V.tensor_tensor(idx_out[:, :], bank[2][:, 0:S], tok_f[:, :], ALU.add))
                V.tensor_scalar(idx_part[:, :], idx_out[:, :], P - 1, None, ALU.bitwise_and)
                then(V.tensor_scalar(idx_tile[:, :], idx_out[:, :], 1, NTOK - P, ALU.logical_shift_right, ALU.bitwise_and))
                V.tensor_tensor(idx_in[:, :], idx_tile[:, :], idx_part[:, :], ALU.add).then_inc(s_idx, 1)
                dv.wait_ge(s_ex, layer + 1)
                then(V.tensor_scalar(den[:, :], ex[:, :], 1.0, None, ALU.add))
                then(V.reciprocal(rden[:, :], den[:, :]))
                then(V.tensor_scalar(gate[:, 0, :], rden[:, :], 0.5, None, ALU.mult))
                then(V.tensor_tensor(gate[:, 1, :], ex[:, :], gate[:, 0, :], ALU.mult))

            def experts(layer):
                base = layer * S
                dv.wait_ge(s_eid, layer + 1)
                dv.wait_ge(s_bias, 32)

                def x_low(n, r, q, e):
                    wait(dv, s_xh, base + n + 1)
                    V.tensor_tensor(xl[:, r % 2, :], bank[r % 2][:, 0:P], xh[:, r % 2, :], ALU.subtract).then_inc(s_xl, 1)

                def bias(n, r, q, e):
                    wait(dv, s_up, base + n + 1)
                    V.tensor_tensor(hb[:, r % 2, :], bank[2 + r % 2][:, :], b1_all[:, bass.ds(e * F, F)], ALU.add).then_inc(s_hb, 1)

                def h_low(n, r, q, e):
                    wait(dv, s_hh, base + n + 1)
                    V.scalar_tensor_tensor(hl[:, r % 2, :], bank[4 + r % 2][:, :], 0.0, hh[:, r % 2, :], ALU.max, ALU.subtract).then_inc(s_hl, 1)

                def y_first(n, r, q, e):
                    wait(dv, s_dn, base + n + 1)
                    V.tensor_tensor(y_high[:, r % 2, :], bank[6 + r % 2][:, 0:D], b2_all[:, bass.ds(e * D, D)], ALU.add).then_inc(s_yh, 1)

                def y(n, r, q, e):
                    wait(dv, s_yh, base + n + 1)
                    wait(dv, s_s[r % YB], 16 * (q + layer * (S // YB)))
                    V.tensor_tensor(yt[:, r % YB, :], bank[6 + r % 2][:, D:2 * D], y_high[:, r % 2, :], ALU.add).then_inc(s_y, 1)

                tile_pipeline(dv, True, [(0, x_low), (UP_AT, bias), (4, y), (2, h_low), (DOWN_AT, y_first)])

            def combine(layer, k):
                def body(u, r, q):
                    if k == 0:
                        before = UNITS // 2 if layer == 1 and r < 2 else 0
                        wait(dv, s_yl[r], 16 * (q + before + 1))
                        if layer == 0:
                            wait(dv, norm["a"]["s_rs"], u - 1)
                    else:
                        wait(dv, s_c0, (u + layer * UNITS + 1) * PT)
                    for j in range(PT):
                        xt = X[:, bass.ds(u * PT + j, 1), :].rearrange("p a d -> p (a d)")
                        V.scalar_tensor_tensor(xt, yb[r][:, j, k, :], gate[:, k, bass.ds(u * PT + j, 1)], xt, ALU.mult, ALU.add).then_inc((s_c0, s_c1)[k], 1)
                return body

            V.memset(cT[R:R + 1, :, :], 1.0).then_inc(s_fix, 1)
            for c in range(GROUPS + 1):
                if c < GROUPS:
                    dv.wait_ge(s_x[c], 16)
                    for t in range(c * GT, (c + 1) * GT):
                        last = V.bn_stats(st0[:, t, :], X[:, t, :])
                    last.then_inc(s_st0, 1)
                    dv.wait_ge(s_st0, c + 1)
                    for t in range(c * GT, (c + 1) * GT):
                        last = V.bn_aggr(mv0[:, t, :], st0[:, t, :])
                    last.then_inc(s_mv0, 1)
                if c > 0:
                    dv.wait_ge(s_pw0, c)
                    for t in range((c - 1) * GT + 1, c * GT, 2):
                        last = V.tensor_scalar(XN0[:, t, :], X[:, t, :], mv0[:, t, 0:1], rs0[:, t:t + 1], ALU.subtract, ALU.mult)
                    last.then_inc(s_xn0[1], 1)
            for c in (0, 1):
                dv.wait_ge(s_wh, c + 1)
                V.tensor_tensor(w_part(c, 1), w_raw(c), w_part(c, 0), ALU.subtract).then_inc(s_split[0], 1)
            dv.wait_ge(s_w, 160)
            dv.wait_ge(s_const, CONSTS)
            route(0)
            wv = wu_raw[:, :].rearrange("r (h s d) -> r s h d", s=2, d=HD)
            for s in range(2):
                last = V.tensor_copy(wu[:, s, :].rearrange("r (h d) -> r h d", d=HD), wv[:, s, :, :])
            last.then_inc(s_wu, 1)
            experts(0)

            def q_(u, r, q):
                wait(dv, s_qe, u + 1)
                wait(dv, s_oz, u - 1)
                V.scalar_tensor_tensor(qT[:, r % 2, :], qe[:, r % 2, :], 1.0, qr[:, r % 2, :], ALU.min, ALU.add).then_inc(s_q, 1)

            def k_(u, r, q):
                wait(dv, s_ke, u + 1)
                wait(dv, s_cp, u - 1)
                V.scalar_tensor_tensor(kk[:, r % 2, :, :], ke[:, r % 2, :, :], 1.0, kr[:, r % 2, :, :], ALU.min, ALU.add).then_inc(s_k, 1)

            def context(u, r, q):
                wait(dv, s_cp, u + 1)
                wait(dv, s_oz, u - 1)
                V.tensor_tensor(cx[:, r % 2, :], bank[4][:, 0:D + H], heads[:, :], ALU.mult).then_inc(s_cx, 1)

            oz = bank[5][:, 0:PT * (D + H)].rearrange("p (t n) -> p t n", t=PT)

            def denominators(u, r, q):
                wait(dv, s_oz, u + 1)
                V.tensor_scalar(zz[:, r, :, :], oz[:, :, D:D + H], 1e-6, None, ALU.add).then_inc(s_zz, 1)

            def reciprocals(u, r, q):
                wait(dv, s_zz, u + 1)
                V.reciprocal(rz[:, r, :, :], zz[:, r, :, :]).then_inc(s_rz, 1)

            def outputs(u, r, q):
                wait(dv, s_rz, u + 1)
                wait(dv, s_oTp, u - 1)
                V.tensor_tensor(on[:, r, :, :].rearrange("p t (h e) -> p t h e", e=HD), oz[:, :, 0:D].rearrange("p t (h e) -> p t h e", e=HD),
                                rz[:, r, :, :].unsqueeze(3).to_broadcast([P, PT, H, HD]), ALU.mult).then_inc(s_on, 1)

            def add_attention(u, r, q):
                xt = X[:, bass.ds(u * PT, PT), :]
                wait(dv, s_pr, u + 1)
                wait(dv, s_xb, u + 1)
                wait(dv, norm["r"]["s_rs"], u - 1)
                V.tensor_tensor(xt, bank[1][:, 0:PT * D].rearrange("p (t d) -> p t d", d=D), xb[:, r, :, :], ALU.add).then_inc(s_x2, 1)

            pipeline(dv, UNITS, 4, 2, [(0, combine(0, 0)), (4, context), (0, combine(0, 1)), (6, statistics("r")),
                                       (3, q_), (0, statistics("a")), (6, await_statistics("r")),
                                       (4, denominators), (6, aggregate("r")), (4, reciprocals), (3, k_),
                                       (0, await_statistics("a")), (4, outputs), (0, aggregate("a")),
                                       (5, add_attention)])
            route(1)
            experts(1)
            pipeline(dv, UNITS, YL, YL, [(0, combine(1, 0)), (1, combine(1, 1))])


_INS = ['L0_attn_x', 'L0_attn_Wq', 'L0_attn_bq', 'L0_attn_Wd', 'L0_attn_bd', 'L0_attn_Wu', 'L0_attn_bu', 'L0_attn_Wo',
        'L0_attn_bo', 'L0_ffn_router_w', 'L0_ffn_router_b', 'L0_ffn_W1', 'L0_ffn_b1', 'L0_ffn_W2', 'L0_ffn_b2']


def kernel(**inputs):
    import numpy as _np
    import concourse.bacc as _bacc
    from concourse import mybir as _mybir
    from concourse.bass_utils import run_bass_kernel_spmd as _run

    nc = _bacc.Bacc("TRN2", target_bir_lowering=False, num_devices=1)
    arrays, args = {}, []
    for name in _INS:
        a = _np.ascontiguousarray(inputs[name])
        arrays[f"in_{name}_dram"] = a
        args.append(nc.dram_tensor(f"in_{name}_dram", a.shape, _mybir.dt.from_np(a.dtype), kind="ExternalInput").ap())
    shape = tuple(inputs['L0_attn_x'].shape)
    args.append(nc.dram_tensor("out_0_dram", shape, _mybir.dt.float32, kind="ExternalOutput").ap())
    build_macaron_block(nc, *args)
    r = _run(nc, [arrays], core_ids=[0])
    return r.results[0]["out_0_dram"]
```
